# Optimizing a Trainium2 kernel written in Bass

```python
import numpy as np
import jax
import jax.numpy as jnp

def _softmax(x, axis=-1):
    return jax.nn.softmax(x, axis=axis)

def _gelu(x):
    return jax.nn.gelu(x, approximate=True)

def _silu(x):
    return jax.nn.silu(x)

def _sigmoid(x):
    return jax.nn.sigmoid(x)

def _layernorm(x, axis=-1, eps=1e-05):
    m = jnp.mean(x, axis=axis, keepdims=True)
    v = jnp.var(x, axis=axis, keepdims=True)
    return (x - m) / jnp.sqrt(v + eps)

def _scatter_add(tgt, idx, src, axis=0):
    return tgt.at[idx].add(src)

def _segment_sum(src, seg, n):
    return jax.ops.segment_sum(src, seg, n)
kernel_name = 'mk_perceiver_d1_seqx_r2_fb670f'

def setup_inputs(seed: int=0):
    np.random.seed(seed)
    _w = jnp.asarray

    def _rec_inputs():
        import jax
        import jax.numpy as jnp
        _rk = jax.random.key(seed)
        x = 7.22e-05 + 1 * jax.random.normal(jax.random.fold_in(_rk, 1), (8, 64, 512), jnp.float32)
        _lenS = 64 - jax.random.randint(jax.random.fold_in(_rk, 7), (8,), 0, max(1, 64 // 4) + 1, jnp.int32)
        _lenS2 = 1601 - jax.random.randint(jax.random.fold_in(_rk, 8), (8,), 0, max(1, 1601 // 4) + 1, jnp.int32)
        _ctx_1024P = jax.random.normal(jax.random.fold_in(_rk, 11), (8, 16, 512), jnp.float32)
        _ctx_1024c = jax.random.dirichlet(jax.random.fold_in(_rk, 511), 0.3 * jnp.ones((16,), jnp.float32), (8, 1601))
        _ctx_1024t = jnp.einsum('bsk,bkd->bsd', _ctx_1024c, _ctx_1024P)
        _ctx_1024t = _ctx_1024t * jax.lax.rsqrt(jnp.mean(jnp.square(_ctx_1024t)) + 1e-12) * 0.953939
        ctx_1024 = 4.13588e-05 + 0.999923 * (_ctx_1024t + 0.3 * jax.random.normal(jax.random.fold_in(_rk, 611), (8, 1601, 512), jnp.float32))
        return (x, ctx_1024)
    x, ctx_1024 = _rec_inputs()

    def _L0_xattn_setup():
        import jax, jax.numpy as jnp
        import numpy as np
        B, S, D_IN, D_MODEL = (4, 1024, 512, 512)
        key = jax.random.key(seed)
        ks = jax.random.split(key, 9)
        return {'q': jax.random.normal(ks[0], (B, S, D_IN), jnp.float32), 'k': jax.random.normal(ks[1], (B, S, D_IN), jnp.float32), 'v': jax.random.normal(ks[2], (B, S, D_IN), jnp.float32), 'Wq': jax.random.normal(ks[3], (D_IN, D_MODEL), jnp.float32) * 0.02, 'bq': jax.random.normal(ks[4], (D_MODEL,), jnp.float32) * 0.02, 'Wk': jax.random.normal(ks[5], (D_IN, D_MODEL), jnp.float32) * 0.02, 'bk': jax.random.normal(ks[6], (D_MODEL,), jnp.float32) * 0.02, 'Wv': jax.random.normal(ks[7], (D_IN, D_MODEL), jnp.float32) * 0.02, 'bv': jax.random.normal(ks[8], (D_MODEL,), jnp.float32) * 0.02}
    _L0_xattn_all = _L0_xattn_setup()
    _L0_xattn_in = {k: v for k, v in _L0_xattn_all.items() if k in ('Wq', 'bq', 'Wk', 'bk', 'Wv', 'bv')}
    del _L0_xattn_all

    def _L0_attn_setup():
        import jax, jax.numpy as jnp
        import numpy as np
        DIM = 512
        HEADS = 16
        HEAD_DIM = DIM // HEADS
        THRESH = 0.29514
        SHARP = 15.0
        LN_EPS = 1e-05
        NORM_EPS = 1e-12

        def _l2norm(t):
            n = jnp.sqrt(jnp.sum(t * t, axis=-1, keepdims=True))
            return t / jnp.maximum(n, NORM_EPS)
        key = jax.random.key(seed)
        ks = jax.random.split(key, 8)
        s = 1.0 / np.sqrt(DIM)
        sg = 1.0 / np.sqrt(HEAD_DIM)
        return {'x': jax.random.normal(ks[0], (2, 1024, DIM), dtype=jnp.float32), 'Wq': jax.random.uniform(ks[1], (DIM, DIM), jnp.float32, -s, s), 'Wk': jax.random.uniform(ks[2], (DIM, DIM), jnp.float32, -s, s), 'Wv': jax.random.uniform(ks[3], (DIM, DIM), jnp.float32, -s, s), 'gq': jax.random.uniform(ks[4], (HEAD_DIM,), jnp.float32, -sg, sg), 'gk': jax.random.uniform(ks[5], (HEAD_DIM,), jnp.float32, -sg, sg), 'Wo': jax.random.uniform(ks[6], (DIM, DIM), jnp.float32, -s, s), 'bo': jax.random.uniform(ks[7], (DIM,), jnp.float32, -s, s), 'ln_w': jnp.ones((DIM,), jnp.float32), 'ln_b': jnp.zeros((DIM,), jnp.float32)}
    _L0_attn_all = _L0_attn_setup()
    _L0_attn_in = {k: v for k, v in _L0_attn_all.items() if k in ('Wq', 'Wk', 'Wv', 'gq', 'gk', 'Wo', 'bo', 'ln_w', 'ln_b')}
    del _L0_attn_all

    def _L0_ffn_setup():
        import jax, jax.numpy as jnp
        import numpy as np
        B, S, H, I, E = (2, 2048, 512, 256, 8)
        key = jax.random.key(seed)
        ks = jax.random.split(key, 5)
        scale_h = 1.0 / np.sqrt(H)
        scale_i = 1.0 / np.sqrt(I)
        return {'hidden_states': jax.random.normal(ks[0], (B, S, H), dtype=jnp.float32), 'gate_w': jax.random.normal(ks[1], (E, H), dtype=jnp.float32) * scale_h, 'w_gate': jax.random.normal(ks[2], (E, I, H), dtype=jnp.float32) * scale_h, 'w_up': jax.random.normal(ks[3], (E, I, H), dtype=jnp.float32) * scale_h, 'w_down': jax.random.normal(ks[4], (E, H, I), dtype=jnp.float32) * scale_i}
    _L0_ffn_all = _L0_ffn_setup()
    _L0_ffn_in = {k: v for k, v in _L0_ffn_all.items() if k in ('gate_w', 'w_gate', 'w_up', 'w_down')}
    del _L0_ffn_all
    return {'x': x, 'ctx_1024': ctx_1024, 'L0_xattn_Wq': _L0_xattn_in['Wq'], 'L0_xattn_bq': _L0_xattn_in['bq'], 'L0_xattn_Wk': _L0_xattn_in['Wk'], 'L0_xattn_bk': _L0_xattn_in['bk'], 'L0_xattn_Wv': _L0_xattn_in['Wv'], 'L0_xattn_bv': _L0_xattn_in['bv'], 'L0_attn_Wq': _L0_attn_in['Wq'], 'L0_attn_Wk': _L0_attn_in['Wk'], 'L0_attn_Wv': _L0_attn_in['Wv'], 'L0_attn_gq': _L0_attn_in['gq'], 'L0_attn_gk': _L0_attn_in['gk'], 'L0_attn_Wo': _L0_attn_in['Wo'], 'L0_attn_bo': _L0_attn_in['bo'], 'L0_attn_ln_w': _L0_attn_in['ln_w'], 'L0_attn_ln_b': _L0_attn_in['ln_b'], 'L0_ffn_gate_w': _L0_ffn_in['gate_w'], 'L0_ffn_w_gate': _L0_ffn_in['w_gate'], 'L0_ffn_w_up': _L0_ffn_in['w_up'], 'L0_ffn_w_down': _L0_ffn_in['w_down']}

def reference(x, ctx_1024, L0_xattn_Wq, L0_xattn_bq, L0_xattn_Wk, L0_xattn_bk, L0_xattn_Wv, L0_xattn_bv, L0_attn_Wq, L0_attn_Wk, L0_attn_Wv, L0_attn_gq, L0_attn_gk, L0_attn_Wo, L0_attn_bo, L0_attn_ln_w, L0_attn_ln_b, L0_ffn_gate_w, L0_ffn_w_gate, L0_ffn_w_up, L0_ffn_w_down):
    import jax
    import jax.numpy as jnp

    def _L0_xattn_ref(q, k, v, Wq, bq, Wk, bk, Wv, bv):
        import jax, jax.numpy as jnp
        import numpy as np
        B, S, D_IN, D_MODEL = (4, 1024, 512, 512)
        qp = jnp.einsum('bsd,de->bse', q, Wq) + bq
        kp = jnp.einsum('bsd,de->bse', k, Wk) + bk
        vp = jnp.einsum('bsd,de->bse', v, Wv) + bv
        scale = 1.0 / jnp.sqrt(jnp.asarray(kp.shape[-1], jnp.float32))
        logits = jnp.einsum('bqe,bke->bqk', qp, kp) * scale
        attn = jax.nn.softmax(logits, axis=-1)
        return jnp.einsum('bqk,bke->bqe', attn, vp)

    def _L0_attn_ref(x, Wq, Wk, Wv, gq, gk, Wo, bo, ln_w, ln_b):
        import jax, jax.numpy as jnp
        import numpy as np
        DIM = 512
        HEADS = 16
        HEAD_DIM = DIM // HEADS
        THRESH = 0.29514
        SHARP = 15.0
        LN_EPS = 1e-05
        NORM_EPS = 1e-12

        def _l2norm(t):
            n = jnp.sqrt(jnp.sum(t * t, axis=-1, keepdims=True))
            return t / jnp.maximum(n, NORM_EPS)
        B, T, D = x.shape
        mu = jnp.mean(x, axis=-1, keepdims=True)
        var = jnp.mean((x - mu) ** 2, axis=-1, keepdims=True)
        x_norm = (x - mu) / jnp.sqrt(var + LN_EPS) * ln_w + ln_b

        def split_heads(t):
            return t.reshape(B, T, HEADS, HEAD_DIM).transpose(0, 2, 1, 3)
        q = _l2norm(split_heads(x_norm @ Wq))
        k = _l2norm(split_heads(x_norm @ Wk))
        v = split_heads(x @ Wv)
        align = jnp.einsum('bhtd,bhsd->bhts', q, k)
        resonance = jax.nn.sigmoid((align - THRESH) * SHARP)
        gate_q = jnp.einsum('bhtd,d->bht', q, gq)
        gate_k = jnp.einsum('bhsd,d->bhs', k, gk)
        modulation = resonance * gate_q[..., :, None] * gate_k[..., None, :]
        collapse = jnp.einsum('bhts,bhsd->bhtd', modulation, v)
        collapse = collapse.transpose(0, 2, 1, 3).reshape(B, T, D)
        return collapse @ Wo + bo

    def _L0_ffn_ref(hidden_states, gate_w, w_gate, w_up, w_down):
        import jax, jax.numpy as jnp
        import numpy as np
        B, S, H, I, E = (2, 2048, 512, 256, 8)
        b, s, h = hidden_states.shape
        x = hidden_states.reshape(-1, h)
        logits = x @ gate_w.T
        top_v = jnp.max(logits, axis=-1)
        sel = jnp.argmax(logits, axis=-1)
        rw = jax.nn.sigmoid(top_v)
        out = jnp.zeros_like(x)
        n_exp = gate_w.shape[0]
        for e in range(n_exp):
            mask = (sel == e).astype(x.dtype)
            xs = x * (rw * mask)[:, None]
            g = xs @ w_gate[e].T
            u = xs @ w_up[e].T
            out = out + u * jax.nn.silu(g) @ w_down[e].T
        return out.reshape(b, s, h)
    x = x + _L0_xattn_ref(_layernorm(x, axis=-1), ctx_1024, ctx_1024, L0_xattn_Wq, L0_xattn_bq, L0_xattn_Wk, L0_xattn_bk, L0_xattn_Wv, L0_xattn_bv)
    x = x + _L0_attn_ref(_layernorm(x, axis=-1), L0_attn_Wq, L0_attn_Wk, L0_attn_Wv, L0_attn_gq, L0_attn_gk, L0_attn_Wo, L0_attn_bo, L0_attn_ln_w, L0_attn_ln_b)
    x = x + _L0_ffn_ref(_layernorm(x, axis=-1), L0_ffn_gate_w, L0_ffn_w_gate, L0_ffn_w_up, L0_ffn_w_down)
    return x

_drawn_inputs = setup_inputs


def setup_inputs(seed=0):
    import zlib

    import numpy as np

    out = dict(_drawn_inputs(seed))
    spreads = {'L0_attn_ln_w': (1.0, 0.6), 'L0_attn_ln_b': (0.0, 0.8)}
    factors = {'L0_xattn_bq': 26.568,
     'L0_xattn_bk': 64.0,
     'L0_attn_Wq': 2.787,
     'L0_attn_Wk': 8.0,
     'L0_attn_Wv': 8.0,
     'L0_attn_gq': 4.586,
     'L0_attn_gk': 3.283,
     'L0_attn_Wo': 8.0,
     'L0_attn_bo': 8.0}
    for name, (base, spread) in spreads.items():
        noise = np.random.default_rng([zlib.crc32(name.encode()), seed]).standard_normal(out[name].shape)
        drawn = base * np.exp(spread * noise) if base else spread * noise
        out[name] = jnp.asarray(drawn.astype(out[name].dtype))
    for name, factor in factors.items():
        out[name] = (out[name] * factor).astype(out[name].dtype)
    return out
```

```python
from contextlib import ExitStack

import concourse.bass as bass
from concourse import mybir

B, S, D = 8, 64, 512
KEYS = 1601
P = 128
DC = D // P
PAIRS = B // 2
FULL = KEYS // P
TAIL = KEYS - FULL * P
KT = FULL + 1
CHUNKS = [(0, 4), (4, 8), (8, FULL), (FULL, KT)]
NCH = len(CHUNKS)
HEADS, HD = 16, 32
HPC = P // HD
THRESH, SHARP = 0.29514, 15.0
EPS = 1e-5
NORM_EPS = 1e-12
E, I = 8, 256
IC = I // P
SLOTS = 96
EROWS = 512
MAXR = -(-EROWS // SLOTS)
OWN = 3
NVEC = 4
ROWV = 2 * D + 2 * HD

STEPS = ("y", "a1", "a2", "q", "k", "gates", "turn", "align0", "align1", "col", "cgT", "o", "h", "route", "rank")
BY_TURNS = {0: ("y",), 5: ("a1",), 7: ("a2",), 9: ("q", "k"), 10: ("gates",), 12: ("turn",)}
BY_SUMS = {0: ("align0", "align1"), 5: ("col",), 7: ("cgT",), 9: ("o",), KT: ("h", "route", "rank")}
TURN, SPREAD = 2, 4
AFTER = dict(zip(STEPS, STEPS[1:] + ("end",)))
LINKS = {"y": 3, "a1": 2, "q": 1, "k": 1, "o": 2, "route": 5, "rank": 2}
LINK_AT = {}
ATT_LINKS = 0
for _step in STEPS:
    LINK_AT[_step] = ATT_LINKS
    ATT_LINKS += LINKS.get(_step, 0)
LINK_AT["end"] = ATT_LINKS
SOFT_LINKS = 4
COUNT_LINKS = 3
ROUND_LINKS = 3 + E


def program(nc, A):
    f32, f16, i32 = mybir.dt.float32, mybir.dt.float16, mybir.dt.int32
    ALU, ACT, AX = mybir.AluOpType, mybir.ActivationFunctionType, mybir.AxisListType
    scale = float(D) ** -0.5
    ctx = ExitStack()
    with ctx:
        def sb(name, shape, dt=f32):
            return ctx.enter_context(nc.sbuf_tensor(name + "_sb", shape, dt))

        def sem(name):
            return ctx.enter_context(nc.semaphore(name))

        CTX = sb("CTX", [P, 2 * KT * D])
        ctxb = CTX[:, :].rearrange("p (k t d) -> p k t d", k=2, t=KT)
        ctxT = sb("ctxT", [P, 2, DC, P])
        iotaS = ctxT[:, :, :, :].rearrange("p a c k -> p (a c k)")[:, 0:E * SLOTS]
        PT = sb("PT", [P, 2 * KT * S])
        probs = PT[:, :].rearrange("p (k t q) -> p k t q", k=2, t=KT)
        pick = PT[:, 0:PAIRS * E * SLOTS // 2].bitcast(f16).rearrange("p (a n) -> p a n", a=PAIRS)
        QK = sb("QK", [P, DC * B * S])
        qk = QK[:, :].rearrange("p (c n) -> p c n", c=DC)
        xsT = QK[:, 0:2 * DC * SLOTS].rearrange("p (a c n) -> p a c n", a=2, c=DC)
        hact = QK[:, 1024:1024 + 2 * IC * SLOTS].rearrange("p (a c n) -> p a c n", a=2, c=IC)
        gate_t = QK[:, 1536:1536 + IC * SLOTS].rearrange("p (c n) -> p c n", c=IC)
        WV = sb("WV", [P, DC * D])
        wv = WV[:, :].rearrange("p (c n) -> p c n", c=DC)
        AW = sb("AW", [P, 3 * DC * D])
        awq, awk, awv = (AW[:, i * DC * D:(i + 1) * DC * D].rearrange("p (c n) -> p c n", c=DC) for i in range(3))
        AO = sb("AO", [P, DC * D])
        awo = AO[:, :].rearrange("p (c n) -> p c n", c=DC)
        WQK = sb("WQK", [P, 2 * DC * D])
        wq = WQK[:, 0:DC * D].rearrange("p (c n) -> p c n", c=DC)
        wkT = WQK[:, DC * D:2 * DC * D].rearrange("p (c n) -> p c n", c=DC)
        qmask = WQK[:, 0:DC * HPC * P].rearrange("p (c j n) -> p c j n", c=DC, j=HPC)
        resbd = WQK[:, DC * D:DC * D + HEADS * P].rearrange("p (h n) -> p h n", h=HEADS)
        XW = DC * 2 * I + IC * D
        FF = sb("FF", [P, OWN * XW])
        xall = FF[:, 0:2048].rearrange("p (a d) -> p a d", a=PAIRS)
        xn = FF[:, 2048:4096].rearrange("p (a d) -> p a d", a=PAIRS)
        xnT = FF[:, 4096:6144].rearrange("p (c n) -> p c n", c=DC)
        qpT = FF[:, 6144:8192].rearrange("p (c n) -> p c n", c=DC)
        places = [(FF[:, e * XW:e * XW + DC * 2 * I], FF[:, e * XW + DC * 2 * I:(e + 1) * XW]) for e in range(OWN)]
        places += [(CTX[:, e * XW:e * XW + DC * 2 * I], CTX[:, e * XW + DC * 2 * I:(e + 1) * XW]) for e in range(4)]
        places += [(WV[:, :], CTX[:, 4 * XW:4 * XW + IC * D])]
        wgu = [g.rearrange("p (c n) -> p c n", c=DC) for g, _ in places]
        wdn = [d.rearrange("p (c n) -> p c n", c=IC) for _, d in places]
        got = [(AW if e < 6 else AO)[0:SLOTS, (e % 6) * 2 * D:(e % 6 + 1) * 2 * D] for e in range(E)]

        def tile(name):
            return sb(name, [P, D])

        qcur = sb("qcur", [P, DC, P])
        pvt = sb("pvt", [P, DC, P])
        xrow, x1, a1, a2, sq, vs, qh, kh = (tile(n) for n in ("xrow", "x1", "a1", "a2", "sq", "vs", "qh", "kh"))
        a1T, a2T, kT = (sb(n, [P, DC, P]) for n in ("a1T", "a2T", "kT"))
        cg, cgT, hT = qh, a1T, a2T
        yout = [a1, a2]
        res = sb("res", [P, DC, HPC * S])
        XR = sb("XR", [P, 2 * D])
        wgate = sb("wgate", [P, DC, 2 * HEADS])
        gwT = sb("gwT", [P, DC, E])
        vec = sb("vec", [P, NVEC, DC])
        rowv = sb("rowv", [P, ROWV])
        bv, bo = rowv[:, 0:D], rowv[:, D:2 * D]
        ident = sb("ident", [P, P])
        ones = sb("ones", [P, P])
        before = sb("before", [P, P], f16)
        ones16 = sb("ones16", [P, P], f16)
        token = sb("token", [P, PAIRS], f16)
        desc = sb("desc", [P, E])
        ebase = sb("ebase", [P, E])
        nhalf = sb("nhalf", [P, 2 * HEADS])
        m1 = sb("m1", [P, S])
        mc = sb("mc", [S, 4])
        diag = sb("diag", [S, S])
        shift = sb("shift", [P, S])
        s1 = sb("s1", [P, 2, S])
        tree = sb("tree", [P, 6, S])
        call = sb("call", [S, B])
        ccur = sb("ccur", [S, 2])
        st = sb("st", [P, 8])
        mv = sb("mv", [P, 2])
        rstd = sb("rstd", [P, 4])
        ss = sb("ss", [P, 2 * HEADS])
        rn = sb("rn", [P, 2 * HEADS])
        gates = sb("gates", [P, 2 * HEADS])
        sm = sb("sm", [P, 8])
        rt = sb("rt", [P, 2, E])
        onehot = sb("onehot", [P, E], f16)
        onesum = sb("onesum", [P, E], f16)
        slot = sb("slot", [P, PAIRS])
        cnt = sb("cnt", [P, 16])
        limits = sb("limits", [P, MAXR - 1])
        tbias = sb("tbias", [P, 1])
        rounds = sb("rounds", [1, 1], i32)
        tok = sb("tok", [SLOTS, 3, E])
        idxg = sb("idxg", [SLOTS, E], i32)
        idxs = sb("idxs", [SLOTS, E], i32)

        def bank(name, n=1):
            return ctx.enter_context(nc.psum_tensor(name, [P, n * 512], f32))

        TR = [bank("TR0"), bank("TR1")]
        LG = bank("LG", 2)
        PV = bank("PV")
        MX = bank("MX")
        A0 = bank("A0")
        A1 = bank("A1")
        AB = [A0, A1]

        def gate_up(e):
            return AB[e % 2][:, 0:2 * IC * SLOTS].rearrange("p (m n) -> p m n", m=2 * IC)

        lgt = LG[:, 0:KT * S].rearrange("p (t q) -> p t q", t=KT)
        pv = PV[:, :].rearrange("p (c n) -> p c n", c=DC)

        scratch = nc.dram_tensor("rows", (B * S, 2 * D), f32, kind="Internal").ap()

        names = """passed x_in wq_in wkT_in vec_in rowv_in wv_in aq_in ak_in av_in awo_in gwT_in
            half_made part_made const_made bias_made ln0_eps ln0_pow xn_made xnT_turned xnT_act xnT_dve
            qp_made qp_moved qk_made qk_moved c_made c_moved gmul gred masks_zeroed
            qcur_made turned t_act t_dve qk_done m1_made m1_turned shift_made shift_spread shift_moved
            shifted probs_made tree_made sums_made pv_chunk pvt_made
            x_loaded xbv_made sum_made y_made x1_made x1b_made var1 pow1 a1_made a1_turned a1T_made
            v_made v_moved var2 pow2 a2_made a2_turned a2T_made q_made q_sq ssq powq qh_made
            k_made k_sq ssk powk kh_made graw_made gates_made vp_made q_turned qmask_act qmask_dve
            k_turned kT_made al_made res_made resbd_made col_made cg_made cg_turned cgT_made
            o_made x2_made var3 pow3 h_made h_turned hT_made lg_made top_made en_made hot_made
            xr_made xr_free rank_made sum_hot slot_made iota_made count_made rounds_made
            pick_made tok_made idx_made x_turned xT_moved gu_made gate_made act_made y2_made yout_made
            pro_chain soft_chain att_chain round_chain""".split()
        s = {n: sem(n) for n in names}
        s_ctx = [[sem(f"ctx_in{k}{c}") for c in range(NCH)] for k in range(2)]
        s_w = [sem(f"expert_in{e}") for e in range(E)]
        s_got = [sem(f"rows_got{e}") for e in range(E)]
        s_stored = [sem(f"out_stored{i}") for i in range(2)]

        block = ctx.enter_context(nc.Block())

        def earlier(eng, name, n):
            if not isinstance(n, int) or n > 0:
                eng.wait_ge(s[name], n)

        def earlier_last(eng, name, n):
            if isinstance(n, int) and n > 0:
                eng.wait_ge(s[name], n)

        def settle(eng):
            eng.sem_inc(s["passed"], 1)

        def turned_bank(bank):
            return bank[:, :].rearrange("p (c n) -> p c n", c=DC)

        @block.sync
        def _(sp):
            def load_ctx(b, k, c):
                lo, hi = CHUNKS[c]
                if c < NCH - 1:
                    src = A["ctx"][bass.ds(b, 1), 0:FULL * P, :].rearrange("a (p t) d -> p (a t) d", t=FULL)[:, lo:hi, :]
                    sp.dma_start(ctxb[:, k, lo:hi, :], src).then_inc(s_ctx[k][c], 16)
                else:
                    src = A["ctx"][bass.ds(b, 1), FULL * P:KEYS, :].rearrange("a p d -> p (a d)")
                    sp.dma_start(ctxb[0:TAIL, k, FULL, :], src).then_inc(s_ctx[k][c], 16)

            def reload_ctx(p, k):
                for c in range(NCH):
                    sp.wait_ge(s["pv_chunk"], NCH * (2 * (p - 1) + k) + c + 1)
                    load_ctx(2 * p + k, k, c)

            def load_weight(dst, name, signal):
                sp.dma_start(dst, A[name].rearrange("(c p) n -> p c n", p=P)).then_inc(s[signal], 16)

            def load_expert(e):
                sp.dma_start(wgu[e], A["wgu"][e]).then_inc(s_w[e], 16)
                sp.dma_start(wdn[e], A["wdn"][e]).then_inc(s_w[e], 16)

            def load_x(p):
                earlier(sp, "x1_made", p)
                sp.dma_start(xrow[:, :], A["x"][bass.ds(p * P, P), :]).then_inc(s["x_loaded"], 16)

            def store_rows(p):
                sp.wait_ge(s["xr_made"], p + 1)
                sp.dma_start(scratch[bass.ds(p * P, P), :], XR[:, :]).then_inc(s["xr_free"], 16)

            sp.sem_inc(s["xr_free"], 16)
            sp.dma_start(xall, A["x"].rearrange("(a p) d -> p a d", p=P)).then_inc(s["x_in"], 16)
            load_weight(wq, "wq", "wq_in")
            load_weight(wkT, "wkT", "wkT_in")
            for c in range(NCH):
                load_ctx(0, 0, c)
            load_weight(awq, "awq", "aq_in")
            load_weight(awk, "awk", "ak_in")
            for c in range(NCH):
                load_ctx(1, 1, c)
            load_weight(wv, "wv", "wv_in")
            load_weight(awv, "awv", "av_in")
            load_weight(awo, "awo", "awo_in")
            load_x(0)
            reload_ctx(1, 0)
            sp.wait_ge(s["qk_moved"], DC)
            sp.wait_ge(s["c_moved"], 1)
            for e in range(OWN):
                load_expert(e)
            with sp.Fori(1, PAIRS - 1) as p:
                reload_ctx(p, 1)
                load_x(p)
                reload_ctx(p + 1, 0)
                store_rows(p - 1)
            reload_ctx(PAIRS - 1, 1)
            load_x(PAIRS - 1)
            store_rows(PAIRS - 2)
            sp.wait_ge(s["pv_chunk"], NCH * B)
            for e in range(OWN, OWN + 4):
                load_expert(e)
            sp.wait_ge(s["y_made"], PAIRS)
            load_expert(E - 1)
            store_rows(PAIRS - 1)
            sp.wait_ge(s["xr_free"], 16 * PAIRS + 16)

        @block.gpsimd
        def _(pool):
            g = nc.gpsimd
            g.memset(nhalf[:], -0.5).then_inc(s["half_made"], 1)
            g.memset(ident[:], 0.0).then_inc(s["part_made"], 1)
            g.memset(before[:], 1.0).then_inc(s["part_made"], 1)
            pool.wait_ge(s["part_made"], 2)
            g.affine_select(out=ident[:], in_=ident[:], compare_op=ALU.not_equal, fill=1.0, base=0,
                            pattern=[[-1, P]], channel_multiplier=1).then_inc(s["const_made"], 1)
            g.affine_select(out=before[:], in_=before[:], compare_op=ALU.is_gt, fill=0.0, base=0,
                            pattern=[[1, P]], channel_multiplier=-1).then_inc(s["const_made"], 1)
            g.memset(ones[:], 1.0).then_inc(s["const_made"], 1)
            g.memset(ones16[:], 1.0).then_inc(s["const_made"], 1)
            g.memset(onesum[:], 0.0).then_inc(s["const_made"], 1)
            loose = dict(channel_multiplier=0, allow_small_or_imprecise_dtypes=True)
            g.iota(desc[:], pattern=[[-1, E]], base=E, **loose).then_inc(s["const_made"], 1)
            g.iota(ebase[:], pattern=[[EROWS, E]], base=0, **loose).then_inc(s["const_made"], 1)
            g.iota(limits[:], pattern=[[SLOTS, MAXR - 1]], base=SLOTS, **loose).then_inc(s["const_made"], 1)
            g.iota(token[:], pattern=[[P, PAIRS]], base=1, channel_multiplier=1,
                   allow_small_or_imprecise_dtypes=True).then_inc(s["const_made"], 1)
            pool.dma_start(vec[:], A["vec"]).then_inc(s["vec_in"], 16)
            pool.dma_start(rowv[:], A["rowv"].partition_broadcast(P)).then_inc(s["rowv_in"], 16)
            pool.dma_start(gwT[:], A["gwT"]).then_inc(s["gwT_in"], 16)
            for t in range(PAIRS):
                pool.wait_ge(s["ln0_eps"], t + 1)
                g.tensor_tensor(rstd[:, t:t + 1], rstd[:, t:t + 1], nhalf[:, 0:1], ALU.pow).then_inc(s["ln0_pow"], 1)
            pool.wait_ge(s["rowv_in"], 16)
            pool.wait_ge(s["aq_in"], 16)
            pool.wait_ge(s["ak_in"], 16)
            for n in range(2 * DC):
                w = (awq, awk)[n // DC][:, n % DC, :].rearrange("p (h d) -> p h d", h=HEADS)
                at = 2 * D + HD * (n // DC)
                gv = rowv[:, at:at + HD].unsqueeze(1).to_broadcast([P, HEADS, HD])
                if n >= 2:
                    pool.wait_ge(s["gred"], n - 1)
                g.tensor_tensor((sq, kh)[n % 2][:, :].rearrange("p (h d) -> p h d", h=HEADS), w, gv, ALU.mult).then_inc(s["gmul"], 1)
            pool.wait_ge(s["qk_made"], DC)
            g.memset(WQK[:], 0.0).then_inc(s["masks_zeroed"], 1)

            def pair_inputs(p):
                pool.wait_ge(s["qk_moved"], DC)
                pool.wait_ge(s["c_moved"], 1)
                earlier(pool, "qk_done", 2 * KT * p)
                earlier(pool, "shift_made", 2 * p)
                g.tensor_copy(qcur[:], qk[:, :, bass.ds(p * P, P)]).then_inc(s["qcur_made"], 1)
                g.tensor_copy(ccur[:], call[:, bass.ds(2 * p, 2)]).then_inc(s["qcur_made"], 1)

            def prob_sums(p, k):
                b = 2 * p + k
                pool.wait_ge(s["probs_made"], 2 * b + 2)
                earlier(pool, "sum_made", p)
                g.tensor_tensor(tree[:], probs[:, k, 0:6, :], probs[:, k, 6:12, :], ALU.add).then_inc(s["tree_made"], 1)
                pool.wait_ge(s["tree_made"], 4 * b + 1)
                g.tensor_tensor(tree[:, 0:3, :], tree[:, 0:3, :], tree[:, 3:6, :], ALU.add).then_inc(s["tree_made"], 1)
                pool.wait_ge(s["tree_made"], 4 * b + 2)
                g.tensor_tensor(tree[:, 0, :], tree[:, 0, :], tree[:, 1, :], ALU.add).then_inc(s["tree_made"], 1)
                pool.wait_ge(s["tree_made"], 4 * b + 3)
                g.tensor_tensor(s1[:, k, :], tree[:, 0, :], tree[:, 2, :], ALU.add).then_inc(s["tree_made"], 1)
                pool.wait_ge(s["tree_made"], 4 * b + 4)
                g.tensor_tensor(s1[0:TAIL, k, :], s1[0:TAIL, k, :], probs[0:TAIL, k, FULL, :], ALU.add).then_inc(s["sums_made"], 1)

            def add_bv(p):
                pool.wait_ge(s["x_loaded"], 16 * p + 16)
                g.tensor_tensor(xrow[:], xrow[:], bv, ALU.add).then_inc(s["xbv_made"], 1)

            def attention(p):
                pool.wait_ge(s["var1"], p + 1)
                g.tensor_tensor(rstd[:, 0:1], rstd[:, 0:1], nhalf[:, 0:1], ALU.pow).then_inc(s["pow1"], 1)
                pool.wait_ge(s["a1_made"], p + 1)
                g.tensor_tensor(x1[:], x1[:], bo, ALU.add).then_inc(s["x1b_made"], 1)
                pool.wait_ge(s["var2"], p + 1)
                g.tensor_tensor(rstd[:, 1:2], rstd[:, 1:2], nhalf[:, 0:1], ALU.pow).then_inc(s["pow2"], 1)
                pool.wait_ge(s["ssq"], p + 1)
                g.tensor_tensor(rn[:, 0:HEADS], ss[:, 0:HEADS], nhalf[:, 0:HEADS], ALU.pow).then_inc(s["powq"], 1)
                pool.wait_ge(s["ssk"], p + 1)
                g.tensor_tensor(rn[:, HEADS:], ss[:, HEADS:], nhalf[:, HEADS:], ALU.pow).then_inc(s["powk"], 1)
                pool.wait_ge(s["gates_made"], p + 1)
                pool.wait_ge(s["v_moved"], p + 1)
                v3 = vs[:, :].rearrange("p (h d) -> p h d", h=HEADS)
                g.tensor_tensor(v3, v3, gates[:, HEADS:].unsqueeze(2).to_broadcast([P, HEADS, HD]), ALU.mult).then_inc(s["vp_made"], 1)
                pool.wait_ge(s["var3"], p + 1)
                g.tensor_tensor(rstd[:, 2:3], rstd[:, 2:3], nhalf[:, 0:1], ALU.pow).then_inc(s["pow3"], 1)
                pool.wait_ge(s["rank_made"], p + 1)
                g.tensor_tensor(onesum[:], onesum[:], onehot[:], ALU.add).then_inc(s["sum_hot"], 1)

            pair_inputs(0)
            prob_sums(0, 0)
            prob_sums(0, 1)
            with pool.Fori(1, PAIRS) as p:
                pair_inputs(p)
                add_bv(p - 1)
                prob_sums(p, 0)
                attention(p - 1)
                prob_sums(p, 1)
            add_bv(PAIRS - 1)
            pool.wait_ge(s["qk_done"], KT * B)
            g.iota(iotaS.rearrange("p (e i) -> p e i", e=E), pattern=[[EROWS, E], [1, SLOTS]], base=0, **loose).then_inc(s["iota_made"], 1)
            attention(PAIRS - 1)

            pool.wait_ge(s["rounds_made"], 1)
            nr = pool.value_load(rounds[0:1, 0:1], min_val=1, max_val=MAXR)
            pool.wait_ge(s["xr_free"], 16 * PAIRS + 16)
            with pool.Fori(0, nr) as r:
                pool.wait_ge(s["idx_made"], 2 * r + 2)
                settle(pool)
                for e in range(E):
                    g.indirect_dma_start(out=got[e], out_offset=None, in_=scratch[:, :],
                                         in_offset=bass.IndirectOffsetOnAxis(ap=idxg[:, e:e + 1], axis=0)).then_inc(s_got[e], 16)
                for e in range(E):
                    pool.wait_ge(s["yout_made"], E * r + e + 1)
                    settle(pool)
                    g.indirect_dma_start(out=A["out"][:, :], out_offset=bass.IndirectOffsetOnAxis(ap=idxs[:, e:e + 1], axis=0),
                                         in_=yout[e % 2][0:SLOTS, :], in_offset=None,
                                         bounds_check=B * S - 1, oob_is_err=False).then_inc(s_stored[e % 2], 16)
                for i in range(2):
                    pool.wait_ge(s_stored[i], 16 * (E // 2) * (r + 1))
                settle(pool)

        @block.scalar
        def _(act):
            a = nc.scalar
            for t in range(0, PAIRS, 2):
                act.wait_ge(s["xnT_turned"], t + 1)
                a.copy(xnT[:, :, t * P:(t + 1) * P], turned_bank(TR[0])).then_inc(s["xnT_act"], 1)
            act.wait_ge(s["vec_in"], 16)
            for m in range(DC):
                act.wait_ge(s["qp_made"], m + 1)
                a.activation(qpT[:, m, :], AB[m % 2][:, :], ACT.Identity, bias=vec[:, 0, m:m + 1]).then_inc(s["qp_moved"], 1)
            for m in range(DC):
                act.wait_ge(s["qk_made"], m + 1)
                a.copy(qk[:, m, :], AB[m % 2][:, :]).then_inc(s["qk_moved"], 1)
            act.wait_ge(s["c_made"], 1)
            a.copy(call[:], MX[0:S, 0:B]).then_inc(s["c_moved"], 1)

            def key_tile(p, i):
                if i % 2:
                    return
                n = 2 * KT * p + i
                w = P if i % KT < FULL else TAIL
                act.wait_ge(s["turned"], n + 1)
                earlier(act, "qk_done", n - 1)
                a.copy(ctxT[:, 0, :, 0:w], turned_bank(TR[0])[:, :, 0:w]).then_inc(s["t_act"], 1)

            def move_shift(b):
                act.wait_ge(s["shift_spread"], b + 1)
                a.copy(shift[:], MX[:, P:P + S]).then_inc(s["shift_moved"], 1)

            def exponentials(b, k):
                act.wait_ge(s["shifted"], 2 * b + 1)
                a.activation(probs[:, k, 0:FULL, :], probs[:, k, 0:FULL, :], ACT.Exp, scale=scale).then_inc(s["probs_made"], 1)
                act.wait_ge(s["shifted"], 2 * b + 2)
                a.activation(probs[0:TAIL, k, FULL, :], probs[0:TAIL, k, FULL, :], ACT.Exp, scale=scale).then_inc(s["probs_made"], 1)

            def move_pvt(p):
                act.wait_ge(s["pv_chunk"], NCH * (2 * p + 2))
                earlier_last(act, "y_made", p)
                a.copy(pvt[:], pv).then_inc(s["pvt_made"], 1)

            def attention(p, step):
                if step == "a1":
                    act.wait_ge(s["a1_turned"], p + 1)
                    a.copy(a1T[:], turned_bank(A1)).then_inc(s["a1T_made"], 1)
                elif step == "a2":
                    act.wait_ge(s["v_made"], p + 1)
                    a.copy(vs[:], A0[:, :]).then_inc(s["v_moved"], 1)
                elif step == "q":
                    act.wait_ge(s["q_made"], p + 1)
                    a.activation(sq[:], A0[:, :], ACT.Square).then_inc(s["q_sq"], 1)
                elif step == "k":
                    act.wait_ge(s["k_made"], p + 1)
                    act.wait_ge(s["ssq"], p + 1)
                    a.activation(sq[:], A1[:, :], ACT.Square).then_inc(s["k_sq"], 1)
                elif step == "turn":
                    act.wait_ge(s["q_turned"], p + 1)
                    for j in range(2):
                        q = slice(HD * j, HD * (j + 1))
                        a.copy(qmask[q, :, j, :], turned_bank(A1)[q, :, :]).then_inc(s["qmask_act"], 1)
                    act.wait_ge(s["k_turned"], p + 1)
                    a.copy(kT[:], turned_bank(A0)).then_inc(s["kT_made"], 1)
                elif step in ("align0", "align1"):
                    half = int(step[-1])
                    act.wait_ge(s["al_made"], 2 * p + half + 1)
                    a.activation(res[:, 2 * half:2 * half + 2, :], AB[1 - half][:, :].rearrange("p (c n) -> p c n", c=2), ACT.Tanh,
                                 scale=SHARP / 2, bias=tbias[:, 0:1]).then_inc(s["res_made"], 1)
                elif step == "cgT":
                    act.wait_ge(s["cg_turned"], p + 1)
                    a.copy(cgT[:], turned_bank(A0)).then_inc(s["cgT_made"], 1)
                elif step == "h":
                    act.wait_ge(s["h_turned"], p + 1)
                    a.copy(hT[:], turned_bank(A0)).then_inc(s["hT_made"], 1)
                elif step == "route":
                    act.wait_ge(s["top_made"], p + 1)
                    a.activation(sm[:, 2:3], sm[:, 0:1], ACT.Exp, scale=-1.0).then_inc(s["en_made"], 1)

            act.wait_ge(s["bias_made"], 1)
            for i in range(KT):
                key_tile(0, i)
            move_shift(0)
            exponentials(0, 0)
            for i in range(KT, 2 * KT):
                key_tile(0, i)
            move_shift(1)
            exponentials(1, 1)
            with act.Fori(1, PAIRS) as p:
                for i in range(KT):
                    key_tile(p, i)
                move_shift(2 * p)
                exponentials(2 * p, 0)
                move_pvt(p - 1)
                for t in range(KT):
                    for step in BY_TURNS.get(t, ()):
                        attention(p - 1, step)
                    key_tile(p, KT + t)
                for t in range(KT + 1):
                    for step in BY_SUMS.get(t, ()):
                        attention(p - 1, step)
                    if t == SPREAD:
                        move_shift(2 * p + 1)
                        exponentials(2 * p + 1, 1)
            move_pvt(PAIRS - 1)
            for step in STEPS:
                attention(PAIRS - 1, step)

            act.wait_ge(s["rounds_made"], 1)
            nr = act.value_load(rounds[0:1, 0:1], min_val=1, max_val=MAXR)
            with act.Fori(0, nr) as r:
                for e in range(E):
                    act.wait_ge(s["gu_made"], E * r + e + 1)
                    if e:
                        act.wait_ge(s["act_made"], E * r + e)
                    a.activation(gate_t[:], gate_up(e)[:, 0:IC, :], ACT.Tanh, scale=0.5).then_inc(s["gate_made"], 1)

        @block.vector
        def _(dve):
            v = nc.vector

            def linker(name, base):
                n = [0]

                def step(ins, settled=False):
                    n[0] += 1
                    ins.then_inc(s[name], 1)
                    dve.wait_ge(s[name], base + n[0])
                    if settled:
                        settle(dve)
                return step, n

            link, _ = linker("pro_chain", 0)
            v.memset(tbias[:], -SHARP * THRESH / 2).then_inc(s["bias_made"], 1)
            dve.wait_ge(s["x_in"], 16)
            dve.wait_ge(s["half_made"], 1)
            for t in range(PAIRS):
                link(v.bn_stats(st[:, 0:6], xall[:, t, :]))
                link(v.bn_aggr(mv[:], st[:, 0:6]))
                v.tensor_scalar(rstd[:, t:t + 1], mv[:, 1:2], EPS, None, ALU.add).then_inc(s["ln0_eps"], 1)
                dve.wait_ge(s["ln0_pow"], t + 1)
                v.tensor_scalar(xn[:, t, :], xall[:, t, :], mv[:, 0:1], rstd[:, t:t + 1], ALU.subtract, ALU.mult).then_inc(s["xn_made"], 1)
            for t in range(1, PAIRS, 2):
                dve.wait_ge(s["xnT_turned"], t + 1)
                v.tensor_copy(xnT[:, :, t * P:(t + 1) * P], turned_bank(TR[1])).then_inc(s["xnT_dve"], 1)
            for n in range(2 * DC):
                dve.wait_ge(s["gmul"], n + 1)
                at = HEADS * (n // DC)
                v.tensor_reduce(wgate[:, n % DC, at:at + HEADS], (sq, kh)[n % 2][:, :].rearrange("p (h d) -> p h d", h=HEADS),
                                AX.X, ALU.add).then_inc(s["gred"], 1)

            def key_tile(p, i):
                if i % 2 == 0:
                    return
                n = 2 * KT * p + i
                w = P if i % KT < FULL else TAIL
                dve.wait_ge(s["turned"], n + 1)
                earlier(dve, "qk_done", n - 1)
                v.tensor_copy(ctxT[:, 1, :, 0:w], turned_bank(TR[1])[:, :, 0:w]).then_inc(s["t_dve"], 1)

            def maxima(b):
                link, _ = linker("soft_chain", SOFT_LINKS * b)
                dve.wait_ge(s["qk_done"], KT * (b + 1))
                link(v.tensor_reduce(m1[:], lgt[:, 0:FULL, :].rearrange("p t q -> p q t"), AX.X, ALU.max))
                v.tensor_tensor(m1[0:TAIL, :], m1[0:TAIL, :], lgt[0:TAIL, FULL, :], ALU.max).then_inc(s["m1_made"], 1)

            def shifts(p, k):
                b = 2 * p + k
                link, n = linker("soft_chain", SOFT_LINKS * b + 1)
                dve.wait_ge(s["m1_turned"], b + 1)
                link(v.tensor_reduce(mc[:, 0:1], MX[0:S, 0:P], AX.X, ALU.max))
                dve.wait_ge(s["qcur_made"], 2 * p + 2)
                link(v.tensor_tensor(mc[:, 1:2], mc[:, 0:1], ccur[:, k:k + 1], ALU.add))
                link(v.tensor_tensor(mc[:, 2:3], ccur[:, k:k + 1], mc[:, 1:2], ALU.subtract))
                v.tensor_scalar(diag[:], ident[0:S, 0:S], mc[:, 2:3], None, ALU.mult).then_inc(s["shift_made"], 1)
                assert n[0] + 1 == SOFT_LINKS

            def shifted(p, k):
                b = 2 * p + k
                dve.wait_ge(s["shift_moved"], b + 1)
                earlier(dve, "pv_chunk", NCH * (b - 1))
                earlier(dve, "sums_made", b - 1)
                v.tensor_tensor(probs[:, k, 0:FULL, :], lgt[:, 0:FULL, :], shift[:].unsqueeze(1).to_broadcast([P, FULL, S]),
                                ALU.add).then_inc(s["shifted"], 1)
                v.tensor_tensor(probs[0:TAIL, k, FULL, :], lgt[0:TAIL, FULL, :], shift[0:TAIL, :], ALU.add).then_inc(s["shifted"], 1)

            def heads(x):
                return x[:, :].rearrange("p (h d) -> p h d", h=HEADS)

            def attention(p, step):
                def start(k):
                    return linker("att_chain", ATT_LINKS * p + LINK_AT[k])

                def statistics(link, x, n, signal):
                    link(v.bn_stats(st[:, 0:6], x), settled=True)
                    link(v.bn_aggr(mv[:], st[:, 0:6]))
                    v.tensor_scalar(rstd[:, n:n + 1], mv[:, 1:2], EPS, None, ALU.add).then_inc(s[signal], 1)

                link, n = start(step)
                if step == "y":
                    dve.wait_ge(s["sum_made"], p + 1)
                    link(v.reciprocal(sm[:, 4:5], A1[:, 0:1]))
                    dve.wait_ge(s["y_made"], p + 1)
                    dve.wait_ge(s["xbv_made"], p + 1)
                    v.scalar_tensor_tensor(out=x1[:], in0=A0[:, :], scalar=sm[:, 4:5], in1=xrow[:], op0=ALU.mult, op1=ALU.add).then_inc(s["x1_made"], 1)
                    dve.wait_ge(s["x1_made"], p + 1)
                    statistics(link, x1[:], 0, "var1")
                elif step == "a1":
                    dve.wait_ge(s["pow1"], p + 1)
                    v.tensor_scalar(a1[:], x1[:], mv[:, 0:1], rstd[:, 0:1], ALU.subtract, ALU.mult).then_inc(s["a1_made"], 1)
                    dve.wait_ge(s["a1_made"], p + 1)
                    statistics(link, a1[:], 1, "var2")
                elif step == "a2":
                    dve.wait_ge(s["pow2"], p + 1)
                    v.tensor_scalar(a2[:], a1[:], mv[:, 0:1], rstd[:, 1:2], ALU.subtract, ALU.mult).then_inc(s["a2_made"], 1)
                    dve.wait_ge(s["a2_turned"], p + 1)
                    for c in range(DC):
                        v.tensor_scalar(a2T[:, c, :], turned_bank(A1)[:, c, :], vec[:, 2, c:c + 1], vec[:, 3, c:c + 1],
                                        ALU.mult, ALU.add).then_inc(s["a2T_made"], 1)
                elif step == "q":
                    dve.wait_ge(s["q_sq"], p + 1)
                    link(v.tensor_reduce(ss[:, 0:HEADS], heads(sq), AX.X, ALU.add))
                    v.tensor_scalar(ss[:, 0:HEADS], ss[:, 0:HEADS], NORM_EPS ** 2, None, ALU.max).then_inc(s["ssq"], 1)
                elif step == "k":
                    dve.wait_ge(s["powq"], p + 1)
                    v.tensor_tensor(heads(qh), heads(A0), rn[:, 0:HEADS].unsqueeze(2).to_broadcast([P, HEADS, HD]), ALU.mult).then_inc(s["qh_made"], 1)
                    dve.wait_ge(s["k_sq"], p + 1)
                    link(v.tensor_reduce(ss[:, HEADS:], heads(sq), AX.X, ALU.add))
                    v.tensor_scalar(ss[:, HEADS:], ss[:, HEADS:], NORM_EPS ** 2, None, ALU.max).then_inc(s["ssk"], 1)
                elif step == "gates":
                    dve.wait_ge(s["powk"], p + 1)
                    v.tensor_tensor(heads(kh), heads(A1), rn[:, HEADS:].unsqueeze(2).to_broadcast([P, HEADS, HD]), ALU.mult).then_inc(s["kh_made"], 1)
                    dve.wait_ge(s["graw_made"], p + 1)
                    v.tensor_tensor(gates[:], A0[:, 0:2 * HEADS], rn[:], ALU.mult).then_inc(s["gates_made"], 1)
                elif step == "turn":
                    dve.wait_ge(s["masks_zeroed"], 1)
                    dve.wait_ge(s["q_turned"], p + 1)
                    for j in range(2, HPC):
                        q = slice(HD * j, HD * (j + 1))
                        v.tensor_copy(qmask[q, :, j, :], turned_bank(A1)[q, :, :]).then_inc(s["qmask_dve"], 1)
                elif step in ("align0", "align1"):
                    half = int(step[-1])
                    dve.wait_ge(s["res_made"], 2 * p + half + 1)
                    for k in range(2):
                        q = slice(S * k, S * (k + 1))
                        v.tensor_scalar(resbd[q, 8 * half:8 * half + 8, q],
                                        res[q, 2 * half:2 * half + 2, :].rearrange("p c (j t) -> p (c j) t", t=S),
                                        1.0, 0.5, ALU.add, ALU.mult).then_inc(s["resbd_made"], 1)
                elif step == "col":
                    dve.wait_ge(s["col_made"], p + 1)
                    v.tensor_tensor(heads(cg), heads(A1), gates[:, 0:HEADS].unsqueeze(2).to_broadcast([P, HEADS, HD]), ALU.mult).then_inc(s["cg_made"], 1)
                elif step == "o":
                    dve.wait_ge(s["o_made"], p + 1)
                    dve.wait_ge(s["x1b_made"], p + 1)
                    dve.wait_ge(s["xr_free"], 16 * p + 16)
                    v.tensor_tensor(XR[:, D:], A1[:, :], x1[:], ALU.add).then_inc(s["x2_made"], 1)
                    dve.wait_ge(s["x2_made"], p + 1)
                    statistics(link, XR[:, D:], 2, "var3")
                elif step == "h":
                    dve.wait_ge(s["pow3"], p + 1)
                    v.tensor_scalar(XR[:, 0:D], XR[:, D:], mv[:, 0:1], rstd[:, 2:3], ALU.subtract, ALU.mult).then_inc(s["h_made"], 1)
                elif step == "route":
                    dve.wait_ge(s["lg_made"], p + 1)
                    v.tensor_reduce(sm[:, 0:1], A1[:, 0:E], AX.X, ALU.max).then_inc(s["top_made"], 1)
                    dve.wait_ge(s["top_made"], p + 1)
                    link(v.tensor_scalar(rt[:, 0, :], A1[:, 0:E], sm[:, 0:1], None, ALU.is_equal))
                    link(v.tensor_tensor(rt[:, 0, :], rt[:, 0, :], desc[:], ALU.mult))
                    link(v.tensor_reduce(sm[:, 1:2], rt[:, 0, :], AX.X, ALU.max))
                    v.tensor_scalar(onehot[:], rt[:, 0, :], sm[:, 1:2], None, ALU.is_equal).then_inc(s["hot_made"], 1)
                    dve.wait_ge(s["en_made"], p + 1)
                    link(v.tensor_scalar(sm[:, 2:3], sm[:, 2:3], 1.0, None, ALU.add))
                    link(v.reciprocal(sm[:, 3:4], sm[:, 2:3]))
                    dve.wait_ge(s["h_turned"], p + 1)
                    v.tensor_scalar(XR[:, 0:D], XR[:, 0:D], sm[:, 3:4], None, ALU.mult).then_inc(s["xr_made"], 1)
                elif step == "rank":
                    dve.wait_ge(s["rank_made"], p + 1)
                    link(v.tensor_tensor(rt[:, 1, :], A0[:, 0:E], ebase[:], ALU.add))
                    link(v.tensor_tensor(rt[:, 1, :], rt[:, 1, :], onehot[:], ALU.mult))
                    v.tensor_reduce(slot[:, bass.ds(p, 1)], rt[:, 1, :], AX.X, ALU.add).then_inc(s["slot_made"], 1)
                    dve.wait_ge(s["sum_hot"], p + 1)
                assert LINK_AT[step] + n[0] == LINK_AT[AFTER[step]]

            dve.wait_ge(s["const_made"], 9)
            dve.wait_ge(s["vec_in"], 16)
            for i in range(KT):
                key_tile(0, i)
            maxima(0)
            shifts(0, 0)
            shifted(0, 0)
            for i in range(KT, 2 * KT):
                key_tile(0, i)
            maxima(1)
            shifts(0, 1)
            shifted(0, 1)
            with dve.Fori(1, PAIRS) as p:
                for i in range(KT):
                    key_tile(p, i)
                maxima(2 * p)
                shifts(p, 0)
                shifted(p, 0)
                for t in range(KT):
                    for step in BY_TURNS.get(t, ()):
                        attention(p - 1, step)
                    key_tile(p, KT + t)
                maxima(2 * p + 1)
                for t in range(KT + 1):
                    for step in BY_SUMS.get(t, ()):
                        attention(p - 1, step)
                    if t == SPREAD:
                        shifts(p, 1)
                        shifted(p, 1)
            for step in STEPS:
                attention(PAIRS - 1, step)

            link, n = linker("round_chain", 0)
            dve.wait_ge(s["count_made"], 1)
            link(v.tensor_reduce(cnt[:, 0:1], A1[:, 0:E], AX.X, ALU.max))
            link(v.tensor_scalar(cnt[:, 2:2 + MAXR - 1], limits[:], cnt[:, 0:1], None, ALU.is_lt))
            link(v.tensor_reduce(cnt[:, 1:2], cnt[:, 2:2 + MAXR - 1], AX.X, ALU.add))
            v.tensor_scalar(rounds[0:1, 0:1], cnt[0:1, 1:2], 1.0, None, ALU.add).then_inc(s["rounds_made"], 1)
            assert n[0] == COUNT_LINKS
            dve.wait_ge(s["rounds_made"], 1)
            dve.wait_ge(s["slot_made"], PAIRS)
            dve.wait_ge(s["iota_made"], 1)
            nr = dve.value_load(rounds[0:1, 0:1], min_val=1, max_val=MAXR)
            with dve.Fori(0, nr) as r:
                link, n = linker("round_chain", COUNT_LINKS + ROUND_LINKS * r)
                for i in range(PAIRS):
                    v.tensor_scalar(pick[:, i, :], iotaS, slot[:, i:i + 1], None, ALU.is_equal).then_inc(s["pick_made"], 1)
                dve.wait_ge(s["pick_made"], PAIRS * r + PAIRS)
                link(v.tensor_scalar(slot[:], slot[:], float(-SLOTS), None, ALU.add))
                dve.wait_ge(s["tok_made"], r + 1)
                link(v.tensor_scalar(tok[:, 0, :], MX[0:SLOTS, 0:E], 0.0, 2.0 * B * S, ALU.is_equal, ALU.mult))
                v.tensor_scalar(idxg[:], MX[0:SLOTS, 0:E], -1.0, 0.0, ALU.add, ALU.max).then_inc(s["idx_made"], 1)
                link(v.tensor_scalar(tok[:, 1, :], MX[0:SLOTS, 0:E], -1.0, None, ALU.add))
                v.tensor_tensor(idxs[:], tok[:, 0, :], tok[:, 1, :], ALU.add).then_inc(s["idx_made"], 1)

                def move_x(e):
                    dve.wait_ge(s["x_turned"], E * r + e + 1)
                    if e >= 2:
                        dve.wait_ge(s["gu_made"], E * r + e - 1)
                    v.tensor_copy(xsT[:, e % 2, :, :], TR[e % 2][:, 0:DC * SLOTS].rearrange("p (c n) -> p c n", c=DC)).then_inc(s["xT_moved"], 1)

                def finish(e):
                    dve.wait_ge(s["y2_made"], E * r + e + 1)
                    if e >= 2:
                        dve.wait_ge(s_stored[e % 2], 16 * ((E // 2) * r + e // 2))
                    v.tensor_tensor(yout[e % 2][0:SLOTS, :], LG[0:SLOTS, 512 * (e % 2):512 * (e % 2) + D], got[e][:, D:], ALU.add).then_inc(s["yout_made"], 1)

                move_x(0)
                for e in range(E):
                    if e + 1 < E:
                        move_x(e + 1)
                    dve.wait_ge(s["gate_made"], E * r + e + 1)
                    link(v.scalar_tensor_tensor(out=gate_t[:], in0=gate_t[:], scalar=1.0, in1=gate_up(e)[:, 0:IC, :], op0=ALU.add, op1=ALU.mult))
                    v.scalar_tensor_tensor(out=hact[:, e % 2, :, :], in0=gate_t[:], scalar=0.5, in1=gate_up(e)[:, IC:, :],
                                           op0=ALU.mult, op1=ALU.mult).then_inc(s["act_made"], 1)
                    if e:
                        finish(e - 1)
                finish(E - 1)
                for i in range(2):
                    dve.wait_ge(s_stored[i], 16 * (E // 2) * (r + 1))
                assert n[0] == ROUND_LINKS

        @block.tensor
        def _(pe):
            t_ = nc.tensor
            pe.wait_ge(s["const_made"], 9)

            def turn_rows(bank, rows, n, w=P):
                for c in range(DC):
                    last = t_.transpose(bank[:, c * w:c * w + n], rows[:, c * P:(c + 1) * P], ident[0:n, 0:n])
                return last

            def project(bank, left, right):
                for c in range(DC):
                    last = t_.matmul(bank[:, :], left[:, c, :], right[:, c, :], start=(c == 0), stop=(c == DC - 1))
                return last

            for t in range(PAIRS):
                pe.wait_ge(s["xn_made"], t + 1)
                earlier(pe, ("xnT_act", "xnT_dve")[t % 2], t // 2)
                turn_rows(TR[t % 2], xn[:, t, :], P).then_inc(s["xnT_turned"], 1)
            pe.wait_ge(s["wq_in"], 16)
            pe.wait_ge(s["xnT_act"], PAIRS // 2)
            pe.wait_ge(s["xnT_dve"], PAIRS // 2)
            for m in range(DC):
                earlier(pe, "qp_moved", m - 1)
                for c in range(DC):
                    last = t_.matmul(AB[m % 2][:, :], wq[:, c, m * P:(m + 1) * P], xnT[:, c, :], start=(c == 0), stop=(c == DC - 1))
                last.then_inc(s["qp_made"], 1)
            pe.wait_ge(s["wkT_in"], 16)
            pe.wait_ge(s["qp_moved"], DC)
            for m in range(DC):
                earlier(pe, "qk_moved", m - 1)
                for c in range(DC):
                    last = t_.matmul(AB[m % 2][:, :], wkT[:, c, m * P:(m + 1) * P], qpT[:, c, :], start=(c == 0), stop=(c == DC - 1))
                last.then_inc(s["qk_made"], 1)
            pe.wait_ge(s["vec_in"], 16)
            for b in range(B):
                for c in range(DC):
                    last = t_.matmul(MX[0:S, b:b + 1], qpT[:, c, b * S:(b + 1) * S], vec[:, 1, c:c + 1], start=(c == 0), stop=(c == DC - 1))
            last.then_inc(s["c_made"], 1)

            def key_tile_turn(p, i):
                n, k, t = 2 * KT * p + i, i // KT, i % KT
                for c, (lo, _) in enumerate(CHUNKS):
                    if t == lo:
                        pe.wait_ge(s_ctx[k][c], 16 * p + 16)
                earlier(pe, ("t_act", "t_dve")[i % 2], KT * p + i // 2)
                w = P if t < FULL else TAIL
                turn_rows(TR[i % 2], ctxb[0:w, k, t, :], w, P).then_inc(s["turned"], 1)

            def scores(p, i):
                k, t = i // KT, i % KT
                w = P if t < FULL else TAIL
                pe.wait_ge(s[("t_act", "t_dve")[i % 2]], KT * p + i // 2 + 1)
                if t == 0:
                    pe.wait_ge(s["qcur_made"], 2 * p + 2)
                    earlier(pe, "shifted", 2 * (2 * p + k))
                for c in range(DC):
                    last = t_.matmul(lgt[0:w, t, :], ctxT[:, i % 2, c, 0:w], qcur[:, c, k * S:(k + 1) * S], start=(c == 0), stop=(c == DC - 1))
                last.then_inc(s["qk_done"], 1)

            def turn_maxima(b):
                pe.wait_ge(s["m1_made"], b + 1)
                if isinstance(b, int) and b == 0:
                    pe.wait_ge(s["c_moved"], 1)
                else:
                    pe.wait_ge(s["shift_moved"], b)
                settle(pe)
                t_.transpose(MX[0:S, 0:P], m1[:], ident[:, :]).then_inc(s["m1_turned"], 1)

            def spread_shifts(b):
                pe.wait_ge(s["shift_made"], b + 1)
                t_.matmul(MX[:, P:P + S], ones[0:S, :], diag[:], start=True, stop=True).then_inc(s["shift_spread"], 1)

            def weigh(p, k, t):
                w = P if t < FULL else TAIL
                b = 2 * p + k
                if t == 0:
                    pe.wait_ge(s["probs_made"], 2 * b + 2)
                    if k == 0:
                        earlier(pe, "pvt_made", p)
                for c in range(DC):
                    last = t_.matmul(pv[:, c, k * S:(k + 1) * S], ctxb[0:w, k, t, c * P:(c + 1) * P], probs[0:w, k, t, :],
                                     start=(t == 0 and c == 0), stop=(t == KT - 1), skip_group_check=True)
                if t + 1 in [hi for _, hi in CHUNKS]:
                    last.then_inc(s["pv_chunk"], 1)

            def attention(p, step):
                if step == "y":
                    pe.wait_ge(s["sums_made"], 2 * p + 2)
                    t_.matmul(A1[:, 0:1], s1[:, :, :].rearrange("p k q -> p (k q)"), ones[:, 0:1], start=True, stop=True).then_inc(s["sum_made"], 1)
                    pe.wait_ge(s["pvt_made"], p + 1)
                    pe.wait_ge(s["wv_in"], 16)
                    earlier_last(pe, "slot_made", p)
                    project(A0, pvt, wv).then_inc(s["y_made"], 1)
                elif step == "a1":
                    pe.wait_ge(s["a1_made"], p + 1)
                    turn_rows(A1, a1, P).then_inc(s["a1_turned"], 1)
                elif step == "a2":
                    pe.wait_ge(s["a1T_made"], p + 1)
                    pe.wait_ge(s["av_in"], 16)
                    project(A0, a1T, awv).then_inc(s["v_made"], 1)
                    pe.wait_ge(s["a2_made"], p + 1)
                    turn_rows(A1, a2, P).then_inc(s["a2_turned"], 1)
                elif step == "q":
                    pe.wait_ge(s["a2T_made"], DC * p + DC)
                    pe.wait_ge(s["v_moved"], p + 1)
                    project(A0, a2T, awq).then_inc(s["q_made"], 1)
                elif step == "k":
                    project(A1, a2T, awk).then_inc(s["k_made"], 1)
                elif step == "gates":
                    pe.wait_ge(s["qh_made"], p + 1)
                    pe.wait_ge(s["gred"], 2 * DC)
                    for c in range(DC):
                        last = t_.matmul(A0[:, 0:2 * HEADS], a2T[:, c, :], wgate[:, c, :], start=(c == 0), stop=(c == DC - 1))
                    last.then_inc(s["graw_made"], 1)
                elif step == "turn":
                    pe.wait_ge(s["kh_made"], p + 1)
                    turn_rows(A1, qh, P).then_inc(s["q_turned"], 1)
                    pe.wait_ge(s["gates_made"], p + 1)
                    turn_rows(A0, kh, P).then_inc(s["k_turned"], 1)
                elif step in ("align0", "align1"):
                    half = int(step[-1])
                    if half == 0:
                        pe.wait_ge(s["qmask_act"], 2 * p + 2)
                        pe.wait_ge(s["qmask_dve"], 2 * p + 2)
                        pe.wait_ge(s["kT_made"], p + 1)
                    for c in range(2 * half, 2 * half + 2):
                        for k in range(2):
                            q = slice(S * k, S * (k + 1))
                            at = (c % 2) * HPC * S
                            last = t_.matmul(AB[1 - half][q, at:at + HPC * S], kT[:, c, q], qmask[:, c, :, q], start=True, stop=True)
                    last.then_inc(s["al_made"], 1)
                elif step == "col":
                    pe.wait_ge(s["resbd_made"], 4 * p + 4)
                    pe.wait_ge(s["vp_made"], p + 1)
                    for h in range(HEADS):
                        last = t_.matmul(A1[:, HD * h:HD * (h + 1)], resbd[:, h, :], vs[:, HD * h:HD * (h + 1)], start=True, stop=True)
                    last.then_inc(s["col_made"], 1)
                elif step == "cgT":
                    pe.wait_ge(s["cg_made"], p + 1)
                    turn_rows(A0, cg, P).then_inc(s["cg_turned"], 1)
                elif step == "o":
                    pe.wait_ge(s["cgT_made"], p + 1)
                    pe.wait_ge(s["awo_in"], 16)
                    project(A1, cgT, awo).then_inc(s["o_made"], 1)
                elif step == "h":
                    pe.wait_ge(s["h_made"], p + 1)
                    turn_rows(A0, XR, P).then_inc(s["h_turned"], 1)
                elif step == "route":
                    pe.wait_ge(s["hT_made"], p + 1)
                    pe.wait_ge(s["gwT_in"], 16)
                    for c in range(DC):
                        last = t_.matmul(A1[:, 0:E], hT[:, c, :], gwT[:, c, :], start=(c == 0), stop=(c == DC - 1))
                    last.then_inc(s["lg_made"], 1)
                elif step == "rank":
                    pe.wait_ge(s["hot_made"], p + 1)
                    earlier_last(pe, "sum_hot", p)
                    t_.matmul(A0[:, 0:E], before[:], onehot[:], start=True, stop=False)
                    t_.matmul(A0[:, 0:E], ones16[:], onesum[:], start=False, stop=True).then_inc(s["rank_made"], 1)

            def turn_and_score(p, k, slots, pa):
                for t in range(KT):
                    for step in slots.get(t, ()):
                        attention(pa, step)
                    if t == 0:
                        key_tile_turn(p, KT * k)
                    if t + 1 < KT:
                        key_tile_turn(p, KT * k + t + 1)
                    scores(p, KT * k + t)

            def weigh_all(p, k, b_next, slots, pa):
                for t in range(KT):
                    for step in slots.get(t, ()):
                        attention(pa, step)
                    if b_next is not None and t == TURN:
                        turn_maxima(b_next)
                    if b_next is not None and t == SPREAD:
                        spread_shifts(b_next)
                    weigh(p, k, t)
                for step in slots.get(KT, ()):
                    attention(pa, step)

            turn_and_score(0, 0, {}, None)
            turn_maxima(0)
            spread_shifts(0)
            turn_and_score(0, 1, {}, None)
            weigh_all(0, 0, 1, {}, None)
            with pe.Fori(1, PAIRS) as p:
                turn_and_score(p, 0, {}, None)
                weigh_all(p - 1, 1, 2 * p, {}, None)
                turn_and_score(p, 1, BY_TURNS, p - 1)
                weigh_all(p, 0, 2 * p + 1, BY_SUMS, p - 1)
            weigh_all(PAIRS - 1, 1, None, {}, None)
            for step in STEPS:
                attention(PAIRS - 1, step)

            pe.wait_ge(s["sum_hot"], PAIRS)
            pe.wait_ge(s["slot_made"], PAIRS)
            t_.matmul(A1[:, 0:E], ones16[:], onesum[:], start=True, stop=True).then_inc(s["count_made"], 1)
            pe.wait_ge(s["rounds_made"], 1)
            nr = pe.value_load(rounds[0:1, 0:1], min_val=1, max_val=MAXR)
            with pe.Fori(0, nr) as r:
                pe.wait_ge(s["pick_made"], PAIRS * r + PAIRS)
                for e in range(E):
                    for i in range(PAIRS):
                        last = t_.matmul(MX[0:SLOTS, e:e + 1], pick[:, i, e * SLOTS:(e + 1) * SLOTS], token[:, i:i + 1],
                                         start=(i == 0), stop=(i == PAIRS - 1))
                last.then_inc(s["tok_made"], 1)

                def turn_x(e):
                    pe.wait_ge(s_got[e], 16 * r + 16)
                    if e >= 2:
                        pe.wait_ge(s["xT_moved"], E * r + e - 1)
                    turn_rows(TR[e % 2], got[e], SLOTS, SLOTS).then_inc(s["x_turned"], 1)

                def down(e):
                    pe.wait_ge(s["act_made"], E * r + e + 1)
                    if e >= 2:
                        pe.wait_ge(s["yout_made"], E * r + e - 1)
                    for c in range(IC):
                        last = t_.matmul(LG[0:SLOTS, 512 * (e % 2):512 * (e % 2) + D], hact[:, e % 2, c, :], wdn[e][:, c, :],
                                         start=(c == 0), stop=(c == IC - 1))
                    last.then_inc(s["y2_made"], 1)

                turn_x(0)
                for e in range(E):
                    if e + 1 < E:
                        turn_x(e + 1)
                    pe.wait_ge(s_w[e], 32)
                    pe.wait_ge(s["xT_moved"], E * r + e + 1)
                    if e >= 2:
                        pe.wait_ge(s["act_made"], E * r + e - 1)
                    for m in range(2 * IC):
                        for c in range(DC):
                            last = t_.matmul(gate_up(e)[:, m, :], wgu[e][:, c, m * P:(m + 1) * P], xsT[:, e % 2, c, :],
                                             start=(c == 0), stop=(c == DC - 1))
                    last.then_inc(s["gu_made"], 1)
                    if e:
                        down(e - 1)
                down(E - 1)


def kernel(**inputs):
    import numpy as np
    import concourse.bacc as bacc
    from concourse.bass_utils import run_bass_kernel_spmd

    x = {k: np.ascontiguousarray(v) for k, v in inputs.items()}

    def column(v):
        return v.reshape(DC, P).T

    wg, wu, wd = (x["L0_ffn_" + n] for n in ("w_gate", "w_up", "w_down"))
    gu = np.concatenate([wg, wu], axis=1).transpose(0, 2, 1)
    dn = wd.transpose(0, 2, 1)
    arrays = {
        "x": x["x"].reshape(B * S, D), "ctx": x["ctx_1024"],
        "wq": x["L0_xattn_Wq"], "wkT": x["L0_xattn_Wk"].T, "wv": x["L0_xattn_Wv"],
        "awq": x["L0_attn_Wq"], "awk": x["L0_attn_Wk"], "awv": x["L0_attn_Wv"], "awo": x["L0_attn_Wo"],
        "vec": np.stack([column(x[n]) for n in ("L0_xattn_bq", "L0_xattn_bk", "L0_attn_ln_w", "L0_attn_ln_b")], axis=1),
        "rowv": np.concatenate([x[n] for n in ("L0_xattn_bv", "L0_attn_bo", "L0_attn_gq", "L0_attn_gk")]),
        "gwT": x["L0_ffn_gate_w"].T.reshape(DC, P, E).transpose(1, 0, 2),
        "wgu": gu.reshape(E, DC, P, 2 * I).transpose(0, 2, 1, 3),
        "wdn": dn.reshape(E, IC, P, D).transpose(0, 2, 1, 3),
    }
    arrays = {k: np.ascontiguousarray(v) for k, v in arrays.items()}
    nc = bacc.Bacc("TRN2", target_bir_lowering=False, num_devices=1)
    A = {k: nc.dram_tensor(k, v.shape, mybir.dt.from_np(v.dtype), kind="ExternalInput").ap() for k, v in arrays.items()}
    A["out"] = nc.dram_tensor("out", (B * S, D), mybir.dt.float32, kind="ExternalOutput").ap()
    program(nc, A)
    r = run_bass_kernel_spmd(nc, [arrays], core_ids=[0])
    return r.results[0]["out"].reshape(B, S, D)
```

```python
from contextlib import ExitStack

import concourse.bass as bass
from concourse import mybir

B, S, D = 8, 64, 512
KEYS = 1601
P = 128
DC = D // P
PAIRS = B // 2
FULL = KEYS // P
TAIL = KEYS - FULL * P
KT = FULL + 1
GT = 2
GROUPS = -(-KT // GT)
CHUNKS = [(0, 4), (4, 8), (8, FULL), (FULL, KT)]
NCH = len(CHUNKS)
HEADS, HD = 16, 32
HPC = P // HD
THRESH, SHARP = 0.29514, 15.0
EPS = 1e-5
NORM_EPS = 1e-12
E, I = 8, 256
IC = I // P
SLOTS = P
EROWS = 512
MAXR = -(-EROWS // SLOTS)
OWN = 2
NVEC = 4
ROWV = 2 * D + 2 * HD

STEPS = ("sum", "on", "y", "a1", "a2", "q", "k", "gates", "turn", "align0", "align1", "col", "cgT", "o", "h", "route", "rank")
BY_SCORES = {0: ("sum",), 1: ("on",), 2: ("y",), 4: ("a1",), 5: ("a2",), 6: ("q", "k"), 7: ("gates",), 8: ("turn",),
             10: ("align0", "align1"), 11: ("col",), 12: ("cgT",), 13: ("o",)}
BY_SUMS = {1: ("h",), 2: ("route",), 3: ("rank",)}
MOVES = KT + NCH // 2
AFTER = dict(zip(STEPS, STEPS[1:] + ("end",)))
LINKS = {"sum": 1, "y": 2, "a1": 2, "q": 1, "k": 1, "o": 2, "route": 5, "rank": 2}
LINK_AT = {}
ATT_LINKS = 0
for _step in STEPS:
    LINK_AT[_step] = ATT_LINKS
    ATT_LINKS += LINKS.get(_step, 0)
LINK_AT["end"] = ATT_LINKS
SOFT_LINKS = NCH + 2
COUNT_LINKS = 3
ROUND_LINKS = 3 + E


def program(nc, A):
    f32, f16, i32 = mybir.dt.float32, mybir.dt.float16, mybir.dt.int32
    ALU, ACT, AX = mybir.AluOpType, mybir.ActivationFunctionType, mybir.AxisListType
    scale = float(D) ** -0.5
    ctx = ExitStack()
    with ctx:
        def sb(name, shape, dt=f32):
            return ctx.enter_context(nc.sbuf_tensor(name + "_sb", shape, dt))

        def sem(name):
            return ctx.enter_context(nc.semaphore(name))

        CTX = sb("CTX", [P, 2 * KT * D])
        ctxb = CTX[:, :].rearrange("p (k t d) -> p k t d", k=2, t=KT)
        CT = sb("CT", [P, 2 * 2 * DC * GT * P])
        ctxT = CT[:, :].rearrange("p (a k c n) -> p a k c n", a=2, k=2, c=DC)
        iotaS = CT[:, 0:E * SLOTS]
        PR = sb("PR", [P, KEYS + KT * P])
        prow = PR[:, 0:KEYS]
        probs = PR[:, KEYS:KEYS + KT * P].rearrange("p (t q) -> p t q", t=KT)
        pick = PR[:, 0:PAIRS * E * SLOTS // 2].bitcast(f16).rearrange("p (a n) -> p a n", a=PAIRS)
        QK = sb("QK", [P, DC * B * S])
        qk = QK[:, :].rearrange("p (c n) -> p c n", c=DC)
        xsT = QK[:, 0:2 * DC * SLOTS].rearrange("p (a c n) -> p a c n", a=2, c=DC)
        hact = QK[:, 1024:1024 + 2 * IC * SLOTS].rearrange("p (a c n) -> p a c n", a=2, c=IC)
        gate_t = QK[:, 1536:1536 + IC * SLOTS].rearrange("p (c n) -> p c n", c=IC)
        WV = sb("WV", [P, DC * D])
        wv = WV[:, :].rearrange("p (c n) -> p c n", c=DC)
        AW = sb("AW", [P, 3 * DC * D])
        awq, awk, awv = (AW[:, i * DC * D:(i + 1) * DC * D].rearrange("p (c n) -> p c n", c=DC) for i in range(3))
        AO = sb("AO", [P, DC * D])
        awo = AO[:, :].rearrange("p (c n) -> p c n", c=DC)
        WQK = sb("WQK", [P, 2 * DC * D])
        wq = WQK[:, 0:DC * D].rearrange("p (c n) -> p c n", c=DC)
        wkT = WQK[:, DC * D:2 * DC * D].rearrange("p (c n) -> p c n", c=DC)
        qmask = WQK[:, 0:DC * HPC * P].rearrange("p (c j n) -> p c j n", c=DC, j=HPC)
        resbd = WQK[:, DC * D:DC * D + HEADS * P].rearrange("p (h n) -> p h n", h=HEADS)
        XW = DC * 2 * I + IC * D
        FF = sb("FF", [P, OWN * XW])
        xall = AW[:, 0:PAIRS * D].rearrange("p (a d) -> p a d", a=PAIRS)
        xn = AW[:, PAIRS * D:2 * PAIRS * D].rearrange("p (a d) -> p a d", a=PAIRS)
        xnT = AW[:, 2 * PAIRS * D:3 * PAIRS * D].rearrange("p (c n) -> p c n", c=DC)
        qpT = AO[:, :].rearrange("p (c n) -> p c n", c=DC)
        places = [(FF[:, e * XW:e * XW + DC * 2 * I], FF[:, e * XW + DC * 2 * I:(e + 1) * XW]) for e in range(OWN)]
        places += [(CTX[:, e * XW:e * XW + DC * 2 * I], CTX[:, e * XW + DC * 2 * I:(e + 1) * XW]) for e in range(4)]
        places += [(WV[:, :], CTX[:, 4 * XW:4 * XW + IC * D])]
        places += [(WQK[:, 0:DC * 2 * I], WQK[:, DC * 2 * I:XW])]
        wgu = [g.rearrange("p (c n) -> p c n", c=DC) for g, _ in places]
        wdn = [d.rearrange("p (c n) -> p c n", c=IC) for _, d in places]
        got = [(AW if e < 6 else AO)[0:SLOTS, (e % 6) * 2 * D:(e % 6 + 1) * 2 * D] for e in range(E)]

        def tile(name):
            return sb(name, [P, D])

        qcur = sb("qcur", [P, DC, P])
        xrow, x1, a1, a2, sq, vs, qh, kh = (tile(n) for n in ("xrow", "x1", "a1", "a2", "sq", "vs", "qh", "kh"))
        on = sq
        a1T, a2T = (sb(n, [P, DC, P]) for n in ("a1T", "a2T"))
        pvt, kT, cgT = a1T, a1T, a1T
        cg, hT = qh, a2T
        yout = [a1, a2]
        res = sb("res", [P, DC, HPC * S])
        XR = sb("XR", [P, 2 * D])
        wgate = sb("wgate", [P, DC, 2 * HEADS])
        gwT = sb("gwT", [P, DC, E])
        vec = sb("vec", [P, NVEC, DC])
        rowv = sb("rowv", [P, ROWV])
        bv, bo = rowv[:, 0:D], rowv[:, D:2 * D]
        ident = sb("ident", [P, P])
        before = sb("before", [P, P], f16)
        ones16 = sb("ones16", [P, P], f16)
        token = sb("token", [P, PAIRS], f16)
        desc = sb("desc", [P, E])
        ebase = sb("ebase", [P, E])
        nhalf = sb("nhalf", [P, 2 * HEADS])
        mx = sb("mx", [P, NCH + 4])
        esum = sb("esum", [P, NCH + 2])
        call = sb("call", [P, PAIRS])
        ccur = sb("ccur", [P, 1])
        st = sb("st", [P, 8])
        mv = sb("mv", [P, 2])
        rstd = sb("rstd", [P, 4])
        ss = sb("ss", [P, 2 * HEADS])
        rn = sb("rn", [P, 2 * HEADS])
        gates = sb("gates", [P, 2 * HEADS])
        sm = sb("sm", [P, 8])
        rt = sb("rt", [P, 2, E])
        onehot = sb("onehot", [P, E], f16)
        onesum = sb("onesum", [P, E], f16)
        slot = sb("slot", [P, PAIRS])
        cnt = sb("cnt", [P, 16])
        limits = sb("limits", [P, MAXR - 1])
        tbias = sb("tbias", [P, 1])
        rounds = sb("rounds", [1, 1], i32)
        tok = sb("tok", [SLOTS, 3, E])
        idxg = sb("idxg", [SLOTS, E], i32)
        idxs = sb("idxs", [SLOTS, E], i32)

        def bank(name, n=1):
            return ctx.enter_context(nc.psum_tensor(name, [P, n * 512], f32))

        TR = [bank("TR0"), bank("TR1")]
        SC = bank("SC", 3)
        ST = bank("ST")
        A0 = bank("A0")
        A1 = bank("A1")
        AB = [A0, A1]

        def gate_up(e):
            return AB[e % 2][:, 0:2 * IC * SLOTS].rearrange("p (m n) -> p m n", m=2 * IC)

        chunk_scores = [SC[:, lo * P:hi * P] for lo, hi in CHUNKS[:-1]] + [ST[:, 0:TAIL]]
        down_bank = [SC[:, 0:D], SC[:, D:2 * D]]

        scratch = nc.dram_tensor("rows", (B * S, 2 * D), f32, kind="Internal").ap()

        names = """passed x_in wq_in wkT_in vec_in rowv_in wv_in aq_in ak_in av_in awo_in gwT_in
            half_made part_made const_made bias_made ln0_eps ln0_pow xn_made xnT_turned xnT_act xnT_dve
            qp_made qp_moved qk_made qk_moved c_made c_moved gmul gred masks_zeroed
            qcur_made turned0 turned1 moved0 moved1 scored shift_made exp_made pv_chunk rsum_made on_made on_turned pvt_made
            x_loaded xbv_made y_made x1_made x1b_made var1 pow1 a1_made a1_turned a1T_made
            v_made v_moved var2 pow2 a2_made a2_turned a2T_made q_made q_sq ssq powq qh_made
            k_made k_sq ssk powk kh_made graw_made gates_made vp_made q_turned qmask_act qmask_dve
            k_turned kT_made al_made res_made resbd_made col_made cg_made cg_turned cgT_made
            o_made x2_made var3 pow3 h_made h_turned hT_made lg_made top_made en_made hot_made
            xr_made xr_free rank_made sum_hot slot_made iota_made count_made rounds_made
            pick_made tok_made idx_made x_turned xT_moved gu_made gate_made act_made y2_made yout_made
            pro_chain soft_chain att_chain round_chain""".split()
        s = {n: sem(n) for n in names}
        s_ctx = [[sem(f"ctx_in{k}{c}") for c in range(NCH)] for k in range(2)]
        s_w = [sem(f"expert_in{e}") for e in range(E)]
        s_got = [sem(f"rows_got{e}") for e in range(E)]
        s_stored = [sem(f"out_stored{i}") for i in range(2)]

        block = ctx.enter_context(nc.Block())

        def earlier(eng, name, n):
            if not isinstance(n, int) or n > 0:
                eng.wait_ge(s[name], n)

        def earlier_last(eng, name, n):
            if isinstance(n, int) and n > 0:
                eng.wait_ge(s[name], n)

        def settle(eng):
            eng.sem_inc(s["passed"], 1)

        def turned_bank(bank):
            return bank[:, :].rearrange("p (c n) -> p c n", c=DC)

        def move_keys(eng, copy, p, k, t):
            if t >= KT:
                return
            grp, w = t // GT, P if t < FULL else TAIL
            eng.wait_ge(s[f"turned{k}"], MOVES * p + t + 1)
            earlier(eng, "scored", GROUPS * p + (grp - 1 if grp else 0))
            copy(ctxT[:, grp % 2, k, :, (t % GT) * P:(t % GT) * P + w], turned_bank(TR[k])[:, :, 0:w]).then_inc(s[f"moved{k}"], 1)

        def move_numerators(eng, copy, p, c):
            lo, hi = CHUNKS[c]
            w = P if c < NCH - 1 else TAIL
            eng.wait_ge(s[f"turned{c % 2}"], MOVES * p + KT + c // 2 + 1)
            copy(probs[0:w, lo:hi, :], TR[c % 2][0:w, 0:(hi - lo) * P].rearrange("p (t q) -> p t q", q=P)).then_inc(s[f"moved{c % 2}"], 1)

        @block.sync
        def _(sp):
            def load_ctx(b, k, c):
                lo, hi = CHUNKS[c]
                if c < NCH - 1:
                    src = A["ctx"][bass.ds(b, 1), 0:FULL * P, :].rearrange("a (p t) d -> p (a t) d", t=FULL)[:, lo:hi, :]
                    sp.dma_start(ctxb[:, k, lo:hi, :], src).then_inc(s_ctx[k][c], 16)
                else:
                    src = A["ctx"][bass.ds(b, 1), FULL * P:KEYS, :].rearrange("a p d -> p (a d)")
                    sp.dma_start(ctxb[0:TAIL, k, FULL, :], src).then_inc(s_ctx[k][c], 16)

            def load_pair(p):
                for c in range(NCH):
                    earlier(sp, "pv_chunk", NCH * (p - 1) + c + 1)
                    for k in range(2):
                        load_ctx(2 * p + k, k, c)

            def load_weight(dst, name, signal):
                sp.dma_start(dst, A[name].rearrange("(c p) n -> p c n", p=P)).then_inc(s[signal], 16)

            def load_expert(e):
                sp.dma_start(wgu[e], A["wgu"][e]).then_inc(s_w[e], 16)
                sp.dma_start(wdn[e], A["wdn"][e]).then_inc(s_w[e], 16)

            def load_x(p):
                earlier(sp, "x1_made", p)
                sp.dma_start(xrow[:, :], A["x"][bass.ds(p * P, P), :]).then_inc(s["x_loaded"], 16)

            def store_rows(p):
                sp.wait_ge(s["xr_made"], p + 1)
                sp.dma_start(scratch[bass.ds(p * P, P), :], XR[:, :]).then_inc(s["xr_free"], 16)

            sp.sem_inc(s["xr_free"], 16)
            sp.dma_start(xall, A["x"].rearrange("(a p) d -> p a d", p=P)).then_inc(s["x_in"], 16)
            load_weight(wq, "wq", "wq_in")
            load_weight(wkT, "wkT", "wkT_in")
            load_x(0)
            load_pair(0)
            load_weight(wv, "wv", "wv_in")
            sp.wait_ge(s["qk_made"], DC)
            sp.wait_ge(s["c_made"], 1)
            load_weight(awv, "awv", "av_in")
            load_weight(awq, "awq", "aq_in")
            load_weight(awk, "awk", "ak_in")
            load_weight(awo, "awo", "awo_in")
            load_pair(1)
            for e in range(OWN):
                load_expert(e)
            with sp.Fori(1, PAIRS - 1) as p:
                load_x(p)
                load_pair(p + 1)
                store_rows(p - 1)
            load_x(PAIRS - 1)
            store_rows(PAIRS - 2)
            sp.wait_ge(s["pv_chunk"], NCH * PAIRS)
            for e in range(OWN, OWN + 4):
                load_expert(e)
            sp.wait_ge(s["y_made"], PAIRS)
            load_expert(OWN + 4)
            sp.wait_ge(s["col_made"], PAIRS)
            load_expert(E - 1)
            store_rows(PAIRS - 1)
            sp.wait_ge(s["xr_free"], 16 * PAIRS + 16)

        @block.gpsimd
        def _(pool):
            g = nc.gpsimd
            g.memset(nhalf[:], -0.5).then_inc(s["half_made"], 1)
            g.memset(ident[:], 0.0).then_inc(s["part_made"], 1)
            g.memset(before[:], 1.0).then_inc(s["part_made"], 1)
            pool.wait_ge(s["part_made"], 2)
            g.affine_select(out=ident[:], in_=ident[:], compare_op=ALU.not_equal, fill=1.0, base=0,
                            pattern=[[-1, P]], channel_multiplier=1).then_inc(s["const_made"], 1)
            g.affine_select(out=before[:], in_=before[:], compare_op=ALU.is_gt, fill=0.0, base=0,
                            pattern=[[1, P]], channel_multiplier=-1).then_inc(s["const_made"], 1)
            g.memset(ones16[:], 1.0).then_inc(s["const_made"], 1)
            g.memset(onesum[:], 0.0).then_inc(s["const_made"], 1)
            loose = dict(channel_multiplier=0, allow_small_or_imprecise_dtypes=True)
            g.iota(desc[:], pattern=[[-1, E]], base=E, **loose).then_inc(s["const_made"], 1)
            g.iota(ebase[:], pattern=[[EROWS, E]], base=0, **loose).then_inc(s["const_made"], 1)
            g.iota(limits[:], pattern=[[SLOTS, MAXR - 1]], base=SLOTS, **loose).then_inc(s["const_made"], 1)
            g.iota(token[:], pattern=[[P, PAIRS]], base=1, channel_multiplier=1,
                   allow_small_or_imprecise_dtypes=True).then_inc(s["const_made"], 1)
            pool.dma_start(vec[:], A["vec"]).then_inc(s["vec_in"], 16)
            pool.dma_start(rowv[:], A["rowv"].partition_broadcast(P)).then_inc(s["rowv_in"], 16)
            pool.dma_start(gwT[:], A["gwT"]).then_inc(s["gwT_in"], 16)
            for t in range(PAIRS):
                pool.wait_ge(s["ln0_eps"], t + 1)
                g.tensor_tensor(rstd[:, t:t + 1], rstd[:, t:t + 1], nhalf[:, 0:1], ALU.pow).then_inc(s["ln0_pow"], 1)
            pool.wait_ge(s["rowv_in"], 16)
            pool.wait_ge(s["aq_in"], 16)
            pool.wait_ge(s["ak_in"], 16)
            for n in range(2 * DC):
                w = (awq, awk)[n // DC][:, n % DC, :].rearrange("p (h d) -> p h d", h=HEADS)
                at = 2 * D + HD * (n // DC)
                gv = rowv[:, at:at + HD].unsqueeze(1).to_broadcast([P, HEADS, HD])
                if n >= 2:
                    pool.wait_ge(s["gred"], n - 1)
                g.tensor_tensor((sq, kh)[n % 2][:, :].rearrange("p (h d) -> p h d", h=HEADS), w, gv, ALU.mult).then_inc(s["gmul"], 1)
            pool.wait_ge(s["qk_made"], DC)
            g.memset(WQK[:], 0.0).then_inc(s["masks_zeroed"], 1)

            def pair_inputs(p):
                pool.wait_ge(s["qk_moved"], DC)
                pool.wait_ge(s["c_moved"], 1)
                earlier(pool, "scored", GROUPS * p)
                earlier(pool, "shift_made", p)
                g.tensor_copy(qcur[:], qk[:, :, bass.ds(p * P, P)]).then_inc(s["qcur_made"], 1)
                g.tensor_copy(ccur[:], call[:, bass.ds(p, 1)]).then_inc(s["qcur_made"], 1)

            def add_bv(p):
                pool.wait_ge(s["x_loaded"], 16 * p + 16)
                g.tensor_tensor(xrow[:], xrow[:], bv, ALU.add).then_inc(s["xbv_made"], 1)

            def attention(p):
                pool.wait_ge(s["var1"], p + 1)
                g.tensor_tensor(rstd[:, 0:1], rstd[:, 0:1], nhalf[:, 0:1], ALU.pow).then_inc(s["pow1"], 1)
                pool.wait_ge(s["a1_made"], p + 1)
                g.tensor_tensor(x1[:], x1[:], bo, ALU.add).then_inc(s["x1b_made"], 1)
                pool.wait_ge(s["var2"], p + 1)
                g.tensor_tensor(rstd[:, 1:2], rstd[:, 1:2], nhalf[:, 0:1], ALU.pow).then_inc(s["pow2"], 1)
                pool.wait_ge(s["ssq"], p + 1)
                g.tensor_tensor(rn[:, 0:HEADS], ss[:, 0:HEADS], nhalf[:, 0:HEADS], ALU.pow).then_inc(s["powq"], 1)
                pool.wait_ge(s["ssk"], p + 1)
                g.tensor_tensor(rn[:, HEADS:], ss[:, HEADS:], nhalf[:, HEADS:], ALU.pow).then_inc(s["powk"], 1)
                pool.wait_ge(s["gates_made"], p + 1)
                pool.wait_ge(s["v_moved"], p + 1)
                v3 = vs[:, :].rearrange("p (h d) -> p h d", h=HEADS)
                g.tensor_tensor(v3, v3, gates[:, HEADS:].unsqueeze(2).to_broadcast([P, HEADS, HD]), ALU.mult).then_inc(s["vp_made"], 1)
                pool.wait_ge(s["var3"], p + 1)
                g.tensor_tensor(rstd[:, 2:3], rstd[:, 2:3], nhalf[:, 0:1], ALU.pow).then_inc(s["pow3"], 1)
                pool.wait_ge(s["rank_made"], p + 1)
                g.tensor_tensor(onesum[:], onesum[:], onehot[:], ALU.add).then_inc(s["sum_hot"], 1)

            pair_inputs(0)
            with pool.Fori(1, PAIRS) as p:
                pair_inputs(p)
                add_bv(p - 1)
                attention(p - 1)
            add_bv(PAIRS - 1)
            pool.wait_ge(s["scored"], GROUPS * PAIRS)
            g.iota(iotaS.rearrange("p (e i) -> p e i", e=E), pattern=[[EROWS, E], [1, SLOTS]], base=0, **loose).then_inc(s["iota_made"], 1)
            attention(PAIRS - 1)

            pool.wait_ge(s["rounds_made"], 1)
            nr = pool.value_load(rounds[0:1, 0:1], min_val=1, max_val=MAXR)
            pool.wait_ge(s["xr_free"], 16 * PAIRS + 16)
            with pool.Fori(0, nr) as r:
                pool.wait_ge(s["idx_made"], 2 * r + 2)
                settle(pool)
                for e in range(E):
                    g.indirect_dma_start(out=got[e], out_offset=None, in_=scratch[:, :],
                                         in_offset=bass.IndirectOffsetOnAxis(ap=idxg[:, e:e + 1], axis=0)).then_inc(s_got[e], 16)
                for e in range(E):
                    pool.wait_ge(s["yout_made"], E * r + e + 1)
                    settle(pool)
                    g.indirect_dma_start(out=A["out"][:, :], out_offset=bass.IndirectOffsetOnAxis(ap=idxs[:, e:e + 1], axis=0),
                                         in_=yout[e % 2][0:SLOTS, :], in_offset=None,
                                         bounds_check=B * S - 1, oob_is_err=False).then_inc(s_stored[e % 2], 16)
                for i in range(2):
                    pool.wait_ge(s_stored[i], 16 * (E // 2) * (r + 1))
                settle(pool)

        @block.scalar
        def _(act):
            a = nc.scalar
            for t in range(0, PAIRS, 2):
                act.wait_ge(s["xnT_turned"], t + 1)
                a.copy(xnT[:, :, t * P:(t + 1) * P], turned_bank(TR[0])).then_inc(s["xnT_act"], 1)
            act.wait_ge(s["vec_in"], 16)
            for m in range(DC):
                act.wait_ge(s["qp_made"], m + 1)
                a.activation(qpT[:, m, :], AB[m % 2][:, :], ACT.Identity, bias=vec[:, 0, m:m + 1]).then_inc(s["qp_moved"], 1)
            for m in range(DC):
                act.wait_ge(s["qk_made"], m + 1)
                a.copy(qk[:, m, :], AB[m % 2][:, :]).then_inc(s["qk_moved"], 1)
            act.wait_ge(s["c_made"], 1)
            a.copy(call[:], ST[:, 0:PAIRS]).then_inc(s["c_moved"], 1)

            def exponentials(p):
                act.wait_ge(s["shift_made"], p + 1)
                earlier(act, "pv_chunk", NCH * p)
                for c, (lo, hi) in enumerate(CHUNKS):
                    keys = slice(lo * P, min(hi * P, KEYS))
                    a.activation(prow[:, keys], chunk_scores[c], ACT.Exp, bias=mx[:, NCH + 2:NCH + 3], scale=scale,
                                 accum_out=esum[:, c:c + 1]).then_inc(s["exp_made"], 1)

            def attention(p, step):
                if step == "sum":
                    act.wait_ge(s["rsum_made"], p + 1)
                    act.wait_ge(s["pv_chunk"], NCH * (p + 1))
                    a.activation(on[:], ST[:, :], ACT.Identity, scale=esum[:, NCH + 1:NCH + 2]).then_inc(s["on_made"], 1)
                elif step == "on":
                    act.wait_ge(s["on_turned"], p + 1)
                    a.copy(pvt[:], turned_bank(A1)).then_inc(s["pvt_made"], 1)
                elif step == "a1":
                    act.wait_ge(s["a1_turned"], p + 1)
                    a.copy(a1T[:], turned_bank(A1)).then_inc(s["a1T_made"], 1)
                elif step == "a2":
                    act.wait_ge(s["v_made"], p + 1)
                    a.copy(vs[:], A0[:, :]).then_inc(s["v_moved"], 1)
                elif step == "q":
                    act.wait_ge(s["q_made"], p + 1)
                    a.activation(sq[:], A0[:, :], ACT.Square).then_inc(s["q_sq"], 1)
                elif step == "k":
                    act.wait_ge(s["k_made"], p + 1)
                    act.wait_ge(s["ssq"], p + 1)
                    a.activation(sq[:], A1[:, :], ACT.Square).then_inc(s["k_sq"], 1)
                elif step == "turn":
                    act.wait_ge(s["q_turned"], p + 1)
                    for j in range(2):
                        q = slice(HD * j, HD * (j + 1))
                        a.copy(qmask[q, :, j, :], turned_bank(A1)[q, :, :]).then_inc(s["qmask_act"], 1)
                    act.wait_ge(s["k_turned"], p + 1)
                    a.copy(kT[:], turned_bank(A0)).then_inc(s["kT_made"], 1)
                elif step in ("align0", "align1"):
                    half = int(step[-1])
                    act.wait_ge(s["al_made"], 2 * p + half + 1)
                    a.activation(res[:, 2 * half:2 * half + 2, :], AB[1 - half][:, :].rearrange("p (c n) -> p c n", c=2), ACT.Tanh,
                                 scale=SHARP / 2, bias=tbias[:, 0:1]).then_inc(s["res_made"], 1)
                elif step == "cgT":
                    act.wait_ge(s["cg_turned"], p + 1)
                    a.copy(cgT[:], turned_bank(A0)).then_inc(s["cgT_made"], 1)
                elif step == "h":
                    act.wait_ge(s["h_turned"], p + 1)
                    a.copy(hT[:], turned_bank(A0)).then_inc(s["hT_made"], 1)
                elif step == "route":
                    act.wait_ge(s["top_made"], p + 1)
                    a.activation(sm[:, 2:3], sm[:, 0:1], ACT.Exp, scale=-1.0).then_inc(s["en_made"], 1)

            act.wait_ge(s["bias_made"], 1)
            for t in range(KT):
                move_keys(act, a.copy, 0, 0, t)
            exponentials(0)
            for c in range(0, NCH, 2):
                move_numerators(act, a.copy, 0, c)
            with act.Fori(1, PAIRS) as p:
                for t in range(GT):
                    move_keys(act, a.copy, p, 0, t)
                for u in range(2 * GROUPS):
                    for step in BY_SCORES.get(u, ()):
                        attention(p - 1, step)
                    move_keys(act, a.copy, p, 0, GT + u)
                exponentials(p)
                for c in range(NCH):
                    for step in BY_SUMS.get(c, ()):
                        attention(p - 1, step)
                    if c % 2 == 0:
                        move_numerators(act, a.copy, p, c)
            for step in STEPS:
                attention(PAIRS - 1, step)

            act.wait_ge(s["rounds_made"], 1)
            nr = act.value_load(rounds[0:1, 0:1], min_val=1, max_val=MAXR)
            with act.Fori(0, nr) as r:
                for e in range(E):
                    act.wait_ge(s["gu_made"], E * r + e + 1)
                    if e:
                        act.wait_ge(s["act_made"], E * r + e)
                    a.activation(gate_t[:], gate_up(e)[:, 0:IC, :], ACT.Tanh, scale=0.5).then_inc(s["gate_made"], 1)

        @block.vector
        def _(dve):
            v = nc.vector

            def linker(name, base):
                n = [0]

                def step(ins, settled=False):
                    n[0] += 1
                    ins.then_inc(s[name], 1)
                    dve.wait_ge(s[name], base + n[0])
                    if settled:
                        settle(dve)
                return step, n

            link, _ = linker("pro_chain", 0)
            v.memset(tbias[:], -SHARP * THRESH / 2).then_inc(s["bias_made"], 1)
            dve.wait_ge(s["x_in"], 16)
            dve.wait_ge(s["half_made"], 1)
            for t in range(PAIRS):
                link(v.bn_stats(st[:, 0:6], xall[:, t, :]))
                link(v.bn_aggr(mv[:], st[:, 0:6]))
                v.tensor_scalar(rstd[:, t:t + 1], mv[:, 1:2], EPS, None, ALU.add).then_inc(s["ln0_eps"], 1)
                dve.wait_ge(s["ln0_pow"], t + 1)
                v.tensor_scalar(xn[:, t, :], xall[:, t, :], mv[:, 0:1], rstd[:, t:t + 1], ALU.subtract, ALU.mult).then_inc(s["xn_made"], 1)
            for t in range(1, PAIRS, 2):
                dve.wait_ge(s["xnT_turned"], t + 1)
                v.tensor_copy(xnT[:, :, t * P:(t + 1) * P], turned_bank(TR[1])).then_inc(s["xnT_dve"], 1)
            for n in range(2 * DC):
                dve.wait_ge(s["gmul"], n + 1)
                at = HEADS * (n // DC)
                v.tensor_reduce(wgate[:, n % DC, at:at + HEADS], (sq, kh)[n % 2][:, :].rearrange("p (h d) -> p h d", h=HEADS),
                                AX.X, ALU.add).then_inc(s["gred"], 1)

            def maximum(p, c, link):
                dve.wait_ge(s["scored"], GROUPS * p + min(CHUNKS[c][1] // GT, GROUPS - 1) + (c == NCH - 1))
                link(v.tensor_reduce(mx[:, c:c + 1], chunk_scores[c], AX.X, ALU.max))

            def shift(p):
                link, n = linker("soft_chain", SOFT_LINKS * p)
                for c in range(NCH):
                    maximum(p, c, link)
                link(v.tensor_reduce(mx[:, NCH:NCH + 1], mx[:, 0:NCH], AX.X, ALU.max))
                dve.wait_ge(s["qcur_made"], 2 * p + 2)
                link(v.tensor_tensor(mx[:, NCH + 1:NCH + 2], mx[:, NCH:NCH + 1], ccur[:], ALU.add))
                v.tensor_scalar(mx[:, NCH + 2:NCH + 3], mx[:, NCH + 1:NCH + 2], ccur[:, 0:1], -scale, ALU.subtract, ALU.mult).then_inc(s["shift_made"], 1)
                assert n[0] == SOFT_LINKS

            def heads(x):
                return x[:, :].rearrange("p (h d) -> p h d", h=HEADS)

            def attention(p, step):
                def start(k):
                    return linker("att_chain", ATT_LINKS * p + LINK_AT[k])

                def statistics(link, x, n, signal):
                    link(v.bn_stats(st[:, 0:6], x), settled=True)
                    link(v.bn_aggr(mv[:], st[:, 0:6]))
                    v.tensor_scalar(rstd[:, n:n + 1], mv[:, 1:2], EPS, None, ALU.add).then_inc(s[signal], 1)

                link, n = start(step)
                if step == "sum":
                    dve.wait_ge(s["exp_made"], NCH * (p + 1))
                    link(v.tensor_reduce(esum[:, NCH:NCH + 1], esum[:, 0:NCH], AX.X, ALU.add))
                    v.reciprocal(esum[:, NCH + 1:NCH + 2], esum[:, NCH:NCH + 1]).then_inc(s["rsum_made"], 1)
                elif step == "y":
                    dve.wait_ge(s["y_made"], p + 1)
                    dve.wait_ge(s["xbv_made"], p + 1)
                    v.tensor_tensor(x1[:], A0[:, :], xrow[:], ALU.add).then_inc(s["x1_made"], 1)
                    dve.wait_ge(s["x1_made"], p + 1)
                    statistics(link, x1[:], 0, "var1")
                elif step == "a1":
                    dve.wait_ge(s["pow1"], p + 1)
                    v.tensor_scalar(a1[:], x1[:], mv[:, 0:1], rstd[:, 0:1], ALU.subtract, ALU.mult).then_inc(s["a1_made"], 1)
                    dve.wait_ge(s["a1_made"], p + 1)
                    statistics(link, a1[:], 1, "var2")
                elif step == "a2":
                    dve.wait_ge(s["pow2"], p + 1)
                    v.tensor_scalar(a2[:], a1[:], mv[:, 0:1], rstd[:, 1:2], ALU.subtract, ALU.mult).then_inc(s["a2_made"], 1)
                    dve.wait_ge(s["a2_turned"], p + 1)
                    for c in range(DC):
                        v.tensor_scalar(a2T[:, c, :], turned_bank(A1)[:, c, :], vec[:, 2, c:c + 1], vec[:, 3, c:c + 1],
                                        ALU.mult, ALU.add).then_inc(s["a2T_made"], 1)
                elif step == "q":
                    dve.wait_ge(s["q_sq"], p + 1)
                    link(v.tensor_reduce(ss[:, 0:HEADS], heads(sq), AX.X, ALU.add))
                    v.tensor_scalar(ss[:, 0:HEADS], ss[:, 0:HEADS], NORM_EPS ** 2, None, ALU.max).then_inc(s["ssq"], 1)
                elif step == "k":
                    dve.wait_ge(s["powq"], p + 1)
                    v.tensor_tensor(heads(qh), heads(A0), rn[:, 0:HEADS].unsqueeze(2).to_broadcast([P, HEADS, HD]), ALU.mult).then_inc(s["qh_made"], 1)
                    dve.wait_ge(s["k_sq"], p + 1)
                    link(v.tensor_reduce(ss[:, HEADS:], heads(sq), AX.X, ALU.add))
                    v.tensor_scalar(ss[:, HEADS:], ss[:, HEADS:], NORM_EPS ** 2, None, ALU.max).then_inc(s["ssk"], 1)
                elif step == "gates":
                    dve.wait_ge(s["powk"], p + 1)
                    v.tensor_tensor(heads(kh), heads(A1), rn[:, HEADS:].unsqueeze(2).to_broadcast([P, HEADS, HD]), ALU.mult).then_inc(s["kh_made"], 1)
                    dve.wait_ge(s["graw_made"], p + 1)
                    v.tensor_tensor(gates[:], A0[:, 0:2 * HEADS], rn[:], ALU.mult).then_inc(s["gates_made"], 1)
                elif step == "turn":
                    dve.wait_ge(s["masks_zeroed"], 1)
                    dve.wait_ge(s["q_turned"], p + 1)
                    for j in range(2, HPC):
                        q = slice(HD * j, HD * (j + 1))
                        v.tensor_copy(qmask[q, :, j, :], turned_bank(A1)[q, :, :]).then_inc(s["qmask_dve"], 1)
                elif step in ("align0", "align1"):
                    half = int(step[-1])
                    dve.wait_ge(s["res_made"], 2 * p + half + 1)
                    for k in range(2):
                        q = slice(S * k, S * (k + 1))
                        v.tensor_scalar(resbd[q, 8 * half:8 * half + 8, q],
                                        res[q, 2 * half:2 * half + 2, :].rearrange("p c (j t) -> p (c j) t", t=S),
                                        1.0, 0.5, ALU.add, ALU.mult).then_inc(s["resbd_made"], 1)
                elif step == "col":
                    dve.wait_ge(s["col_made"], p + 1)
                    v.tensor_tensor(heads(cg), heads(A1), gates[:, 0:HEADS].unsqueeze(2).to_broadcast([P, HEADS, HD]), ALU.mult).then_inc(s["cg_made"], 1)
                elif step == "o":
                    dve.wait_ge(s["o_made"], p + 1)
                    dve.wait_ge(s["x1b_made"], p + 1)
                    dve.wait_ge(s["xr_free"], 16 * p + 16)
                    v.tensor_tensor(XR[:, D:], A1[:, :], x1[:], ALU.add).then_inc(s["x2_made"], 1)
                    dve.wait_ge(s["x2_made"], p + 1)
                    statistics(link, XR[:, D:], 2, "var3")
                elif step == "h":
                    dve.wait_ge(s["pow3"], p + 1)
                    v.tensor_scalar(XR[:, 0:D], XR[:, D:], mv[:, 0:1], rstd[:, 2:3], ALU.subtract, ALU.mult).then_inc(s["h_made"], 1)
                elif step == "route":
                    dve.wait_ge(s["lg_made"], p + 1)
                    v.tensor_reduce(sm[:, 0:1], A1[:, 0:E], AX.X, ALU.max).then_inc(s["top_made"], 1)
                    dve.wait_ge(s["top_made"], p + 1)
                    link(v.tensor_scalar(rt[:, 0, :], A1[:, 0:E], sm[:, 0:1], None, ALU.is_equal))
                    link(v.tensor_tensor(rt[:, 0, :], rt[:, 0, :], desc[:], ALU.mult))
                    link(v.tensor_reduce(sm[:, 1:2], rt[:, 0, :], AX.X, ALU.max))
                    v.tensor_scalar(onehot[:], rt[:, 0, :], sm[:, 1:2], None, ALU.is_equal).then_inc(s["hot_made"], 1)
                    dve.wait_ge(s["en_made"], p + 1)
                    link(v.tensor_scalar(sm[:, 2:3], sm[:, 2:3], 1.0, None, ALU.add))
                    link(v.reciprocal(sm[:, 3:4], sm[:, 2:3]))
                    dve.wait_ge(s["h_turned"], p + 1)
                    v.tensor_scalar(XR[:, 0:D], XR[:, 0:D], sm[:, 3:4], None, ALU.mult).then_inc(s["xr_made"], 1)
                elif step == "rank":
                    dve.wait_ge(s["rank_made"], p + 1)
                    link(v.tensor_tensor(rt[:, 1, :], A0[:, 0:E], ebase[:], ALU.add))
                    link(v.tensor_tensor(rt[:, 1, :], rt[:, 1, :], onehot[:], ALU.mult))
                    v.tensor_reduce(slot[:, bass.ds(p, 1)], rt[:, 1, :], AX.X, ALU.add).then_inc(s["slot_made"], 1)
                    dve.wait_ge(s["sum_hot"], p + 1)
                assert LINK_AT[step] + n[0] == LINK_AT[AFTER[step]]

            dve.wait_ge(s["const_made"], 8)
            dve.wait_ge(s["vec_in"], 16)
            for t in range(KT):
                move_keys(dve, v.tensor_copy, 0, 1, t)
            shift(0)
            for c in range(1, NCH, 2):
                move_numerators(dve, v.tensor_copy, 0, c)
            with dve.Fori(1, PAIRS) as p:
                for t in range(GT):
                    move_keys(dve, v.tensor_copy, p, 1, t)
                for u in range(2 * GROUPS):
                    for step in BY_SCORES.get(u, ()):
                        attention(p - 1, step)
                    move_keys(dve, v.tensor_copy, p, 1, GT + u)
                shift(p)
                for c in range(NCH):
                    for step in BY_SUMS.get(c, ()):
                        attention(p - 1, step)
                    if c % 2:
                        move_numerators(dve, v.tensor_copy, p, c)
            for step in STEPS:
                attention(PAIRS - 1, step)

            link, n = linker("round_chain", 0)
            dve.wait_ge(s["count_made"], 1)
            link(v.tensor_reduce(cnt[:, 0:1], A1[:, 0:E], AX.X, ALU.max))
            link(v.tensor_scalar(cnt[:, 2:2 + MAXR - 1], limits[:], cnt[:, 0:1], None, ALU.is_lt))
            link(v.tensor_reduce(cnt[:, 1:2], cnt[:, 2:2 + MAXR - 1], AX.X, ALU.add))
            v.tensor_scalar(rounds[0:1, 0:1], cnt[0:1, 1:2], 1.0, None, ALU.add).then_inc(s["rounds_made"], 1)
            assert n[0] == COUNT_LINKS
            dve.wait_ge(s["rounds_made"], 1)
            dve.wait_ge(s["slot_made"], PAIRS)
            dve.wait_ge(s["iota_made"], 1)
            nr = dve.value_load(rounds[0:1, 0:1], min_val=1, max_val=MAXR)
            with dve.Fori(0, nr) as r:
                link, n = linker("round_chain", COUNT_LINKS + ROUND_LINKS * r)
                for i in range(PAIRS):
                    v.tensor_scalar(pick[:, i, :], iotaS, slot[:, i:i + 1], None, ALU.is_equal).then_inc(s["pick_made"], 1)
                dve.wait_ge(s["pick_made"], PAIRS * r + PAIRS)
                link(v.tensor_scalar(slot[:], slot[:], float(-SLOTS), None, ALU.add))
                dve.wait_ge(s["tok_made"], r + 1)
                link(v.tensor_scalar(tok[:, 0, :], ST[0:SLOTS, 0:E], 0.0, 2.0 * B * S, ALU.is_equal, ALU.mult))
                v.tensor_scalar(idxg[:], ST[0:SLOTS, 0:E], -1.0, 0.0, ALU.add, ALU.max).then_inc(s["idx_made"], 1)
                link(v.tensor_scalar(tok[:, 1, :], ST[0:SLOTS, 0:E], -1.0, None, ALU.add))
                v.tensor_tensor(idxs[:], tok[:, 0, :], tok[:, 1, :], ALU.add).then_inc(s["idx_made"], 1)

                def move_x(e):
                    dve.wait_ge(s["x_turned"], E * r + e + 1)
                    if e >= 2:
                        dve.wait_ge(s["gu_made"], E * r + e - 1)
                    v.tensor_copy(xsT[:, e % 2, :, :], TR[e % 2][:, 0:DC * SLOTS].rearrange("p (c n) -> p c n", c=DC)).then_inc(s["xT_moved"], 1)

                def finish(e):
                    dve.wait_ge(s["y2_made"], E * r + e + 1)
                    if e >= 2:
                        dve.wait_ge(s_stored[e % 2], 16 * ((E // 2) * r + e // 2))
                    v.tensor_tensor(yout[e % 2][0:SLOTS, :], down_bank[e % 2][0:SLOTS, :], got[e][:, D:], ALU.add).then_inc(s["yout_made"], 1)

                move_x(0)
                for e in range(E):
                    if e + 1 < E:
                        move_x(e + 1)
                    dve.wait_ge(s["gate_made"], E * r + e + 1)
                    link(v.scalar_tensor_tensor(out=gate_t[:], in0=gate_t[:], scalar=1.0, in1=gate_up(e)[:, 0:IC, :], op0=ALU.add, op1=ALU.mult))
                    v.scalar_tensor_tensor(out=hact[:, e % 2, :, :], in0=gate_t[:], scalar=0.5, in1=gate_up(e)[:, IC:, :],
                                           op0=ALU.mult, op1=ALU.mult).then_inc(s["act_made"], 1)
                    if e:
                        finish(e - 1)
                finish(E - 1)
                for i in range(2):
                    dve.wait_ge(s_stored[i], 16 * (E // 2) * (r + 1))
                assert n[0] == ROUND_LINKS

        @block.tensor
        def _(pe):
            t_ = nc.tensor
            pe.wait_ge(s["const_made"], 8)

            def turn_rows(bank, rows, n, w=P):
                for c in range(DC):
                    last = t_.transpose(bank[:, c * w:c * w + n], rows[:, c * P:(c + 1) * P], ident[0:n, 0:n])
                return last

            def project(bank, left, right):
                for c in range(DC):
                    last = t_.matmul(bank[:, :], left[:, c, :], right[:, c, :], start=(c == 0), stop=(c == DC - 1))
                return last

            for t in range(PAIRS):
                pe.wait_ge(s["xn_made"], t + 1)
                earlier(pe, ("xnT_act", "xnT_dve")[t % 2], t // 2)
                turn_rows(TR[t % 2], xn[:, t, :], P).then_inc(s["xnT_turned"], 1)
            pe.wait_ge(s["wq_in"], 16)
            pe.wait_ge(s["xnT_act"], PAIRS // 2)
            pe.wait_ge(s["xnT_dve"], PAIRS // 2)
            for m in range(DC):
                earlier(pe, "qp_moved", m - 1)
                for c in range(DC):
                    last = t_.matmul(AB[m % 2][:, :], wq[:, c, m * P:(m + 1) * P], xnT[:, c, :], start=(c == 0), stop=(c == DC - 1))
                last.then_inc(s["qp_made"], 1)
            pe.wait_ge(s["wkT_in"], 16)
            pe.wait_ge(s["qp_moved"], DC)
            for m in range(DC):
                earlier(pe, "qk_moved", m - 1)
                for c in range(DC):
                    last = t_.matmul(AB[m % 2][:, :], wkT[:, c, m * P:(m + 1) * P], qpT[:, c, :], start=(c == 0), stop=(c == DC - 1))
                last.then_inc(s["qk_made"], 1)
            pe.wait_ge(s["vec_in"], 16)
            for p in range(PAIRS):
                for c in range(DC):
                    last = t_.matmul(ST[:, p:p + 1], qpT[:, c, p * P:(p + 1) * P], vec[:, 1, c:c + 1], start=(c == 0), stop=(c == DC - 1))
            last.then_inc(s["c_made"], 1)

            def turn_keys(p, t):
                if t >= KT:
                    return
                w = P if t < FULL else TAIL
                for k in range(2):
                    for c, (lo, _) in enumerate(CHUNKS):
                        if t == lo:
                            pe.wait_ge(s_ctx[k][c], 16 * p + 16)
                    earlier(pe, f"moved{k}", MOVES * p + t)
                    turn_rows(TR[k], ctxb[0:w, k, t, :], w, P).then_inc(s[f"turned{k}"], 1)

            def score(p, grp, half):
                lo, n = grp * GT, GT * P if grp < GROUPS - 1 else TAIL
                if half == 0:
                    for k in range(2):
                        pe.wait_ge(s[f"moved{k}"], MOVES * p + min(lo + GT, KT))
                    if grp == 0:
                        pe.wait_ge(s["qcur_made"], 2 * p + 2)
                        earlier(pe, "exp_made", NCH * p)
                    if grp == GROUPS - 1:
                        earlier(pe, "on_made", p)
                        if isinstance(p, int) and p == 0:
                            pe.wait_ge(s["c_moved"], 1)
                out = SC[:, lo * P:lo * P + n] if grp < GROUPS - 1 else ST[:, 0:n]
                for c in range(2 * half, 2 * half + 2):
                    for k in range(2):
                        q = slice(k * S, (k + 1) * S)
                        last = t_.matmul(out[q, :], qcur[:, c, q], ctxT[:, grp % 2, k, c, 0:n], start=(c == 0), stop=(c == DC - 1))
                if half == 1:
                    last.then_inc(s["scored"], 1)

            def turn_numerators(p, c):
                lo, hi = CHUNKS[c]
                pe.wait_ge(s["exp_made"], NCH * p + c + 1)
                pe.wait_ge(s[f"moved{c % 2}"], MOVES * p + KT + c // 2)
                for t in range(lo, hi):
                    w = P if t < FULL else TAIL
                    last = t_.transpose(TR[c % 2][0:w, (t - lo) * P:(t - lo + 1) * P], prow[:, t * P:t * P + w], ident[:, :])
                last.then_inc(s[f"turned{c % 2}"], 1)

            def weigh(p, c):
                lo, hi = CHUNKS[c]
                pe.wait_ge(s[f"moved{c % 2}"], MOVES * p + KT + c // 2 + 1)
                if c == 0:
                    pe.wait_ge(s["exp_made"], NCH * (p + 1))
                for t in range(lo, hi):
                    w = P if t < FULL else TAIL
                    for k in range(2):
                        q = slice(k * S, (k + 1) * S)
                        last = t_.matmul(ST[q, :], probs[0:w, t, q], ctxb[0:w, k, t, :], start=(t == 0), stop=(t == KT - 1))
                last.then_inc(s["pv_chunk"], 1)

            def attention(p, step):
                if step == "on":
                    pe.wait_ge(s["on_made"], p + 1)
                    turn_rows(A1, on, P).then_inc(s["on_turned"], 1)
                elif step == "y":
                    pe.wait_ge(s["pvt_made"], p + 1)
                    pe.wait_ge(s["wv_in"], 16)
                    earlier_last(pe, "slot_made", p)
                    project(A0, pvt, wv).then_inc(s["y_made"], 1)
                elif step == "a1":
                    pe.wait_ge(s["a1_made"], p + 1)
                    turn_rows(A1, a1, P).then_inc(s["a1_turned"], 1)
                elif step == "a2":
                    pe.wait_ge(s["a1T_made"], p + 1)
                    pe.wait_ge(s["av_in"], 16)
                    project(A0, a1T, awv).then_inc(s["v_made"], 1)
                    pe.wait_ge(s["a2_made"], p + 1)
                    turn_rows(A1, a2, P).then_inc(s["a2_turned"], 1)
                elif step == "q":
                    pe.wait_ge(s["a2T_made"], DC * p + DC)
                    pe.wait_ge(s["v_moved"], p + 1)
                    project(A0, a2T, awq).then_inc(s["q_made"], 1)
                elif step == "k":
                    project(A1, a2T, awk).then_inc(s["k_made"], 1)
                elif step == "gates":
                    pe.wait_ge(s["qh_made"], p + 1)
                    pe.wait_ge(s["gred"], 2 * DC)
                    for c in range(DC):
                        last = t_.matmul(A0[:, 0:2 * HEADS], a2T[:, c, :], wgate[:, c, :], start=(c == 0), stop=(c == DC - 1))
                    last.then_inc(s["graw_made"], 1)
                elif step == "turn":
                    pe.wait_ge(s["kh_made"], p + 1)
                    turn_rows(A1, qh, P).then_inc(s["q_turned"], 1)
                    pe.wait_ge(s["gates_made"], p + 1)
                    turn_rows(A0, kh, P).then_inc(s["k_turned"], 1)
                elif step in ("align0", "align1"):
                    half = int(step[-1])
                    if half == 0:
                        pe.wait_ge(s["qmask_act"], 2 * p + 2)
                        pe.wait_ge(s["qmask_dve"], 2 * p + 2)
                        pe.wait_ge(s["kT_made"], p + 1)
                    for c in range(2 * half, 2 * half + 2):
                        for k in range(2):
                            q = slice(S * k, S * (k + 1))
                            at = (c % 2) * HPC * S
                            last = t_.matmul(AB[1 - half][q, at:at + HPC * S], kT[:, c, q], qmask[:, c, :, q], start=True, stop=True)
                    last.then_inc(s["al_made"], 1)
                elif step == "col":
                    pe.wait_ge(s["resbd_made"], 4 * p + 4)
                    pe.wait_ge(s["vp_made"], p + 1)
                    for h in range(HEADS):
                        last = t_.matmul(A1[:, HD * h:HD * (h + 1)], resbd[:, h, :], vs[:, HD * h:HD * (h + 1)], start=True, stop=True)
                    last.then_inc(s["col_made"], 1)
                elif step == "cgT":
                    pe.wait_ge(s["cg_made"], p + 1)
                    turn_rows(A0, cg, P).then_inc(s["cg_turned"], 1)
                elif step == "o":
                    pe.wait_ge(s["cgT_made"], p + 1)
                    pe.wait_ge(s["awo_in"], 16)
                    project(A1, cgT, awo).then_inc(s["o_made"], 1)
                elif step == "h":
                    pe.wait_ge(s["h_made"], p + 1)
                    turn_rows(A0, XR, P).then_inc(s["h_turned"], 1)
                elif step == "route":
                    pe.wait_ge(s["hT_made"], p + 1)
                    pe.wait_ge(s["gwT_in"], 16)
                    for c in range(DC):
                        last = t_.matmul(A1[:, 0:E], hT[:, c, :], gwT[:, c, :], start=(c == 0), stop=(c == DC - 1))
                    last.then_inc(s["lg_made"], 1)
                elif step == "rank":
                    pe.wait_ge(s["hot_made"], p + 1)
                    earlier_last(pe, "sum_hot", p)
                    t_.matmul(A0[:, 0:E], before[:], onehot[:], start=True, stop=False)
                    t_.matmul(A0[:, 0:E], ones16[:], onesum[:], start=False, stop=True).then_inc(s["rank_made"], 1)

            def scores(p, pa):
                turn_keys(p, 0)
                turn_keys(p, 1)
                for u in range(2 * GROUPS):
                    if pa is not None:
                        for step in BY_SCORES.get(u, ()):
                            attention(pa, step)
                    turn_keys(p, GT + u)
                    score(p, u // 2, u % 2)

            def sums(p, pa):
                turn_numerators(p, 0)
                for c in range(NCH):
                    if pa is not None:
                        for step in BY_SUMS.get(c, ()):
                            attention(pa, step)
                    if c + 1 < NCH:
                        turn_numerators(p, c + 1)
                    weigh(p, c)

            scores(0, None)
            sums(0, None)
            with pe.Fori(1, PAIRS) as p:
                scores(p, p - 1)
                sums(p, p - 1)
            for step in STEPS:
                attention(PAIRS - 1, step)

            pe.wait_ge(s["sum_hot"], PAIRS)
            pe.wait_ge(s["slot_made"], PAIRS)
            t_.matmul(A1[:, 0:E], ones16[:], onesum[:], start=True, stop=True).then_inc(s["count_made"], 1)
            pe.wait_ge(s["rounds_made"], 1)
            nr = pe.value_load(rounds[0:1, 0:1], min_val=1, max_val=MAXR)
            with pe.Fori(0, nr) as r:
                pe.wait_ge(s["pick_made"], PAIRS * r + PAIRS)
                for e in range(E):
                    for i in range(PAIRS):
                        last = t_.matmul(ST[0:SLOTS, e:e + 1], pick[:, i, e * SLOTS:(e + 1) * SLOTS], token[:, i:i + 1],
                                         start=(i == 0), stop=(i == PAIRS - 1))
                last.then_inc(s["tok_made"], 1)

                def turn_x(e):
                    pe.wait_ge(s_got[e], 16 * r + 16)
                    if e >= 2:
                        pe.wait_ge(s["xT_moved"], E * r + e - 1)
                    turn_rows(TR[e % 2], got[e], SLOTS, SLOTS).then_inc(s["x_turned"], 1)

                def down(e):
                    pe.wait_ge(s["act_made"], E * r + e + 1)
                    if e >= 2:
                        pe.wait_ge(s["yout_made"], E * r + e - 1)
                    for c in range(IC):
                        last = t_.matmul(down_bank[e % 2][0:SLOTS, :], hact[:, e % 2, c, :], wdn[e][:, c, :],
                                         start=(c == 0), stop=(c == IC - 1))
                    last.then_inc(s["y2_made"], 1)

                turn_x(0)
                for e in range(E):
                    if e + 1 < E:
                        turn_x(e + 1)
                    pe.wait_ge(s_w[e], 32)
                    pe.wait_ge(s["xT_moved"], E * r + e + 1)
                    if e >= 2:
                        pe.wait_ge(s["act_made"], E * r + e - 1)
                    for m in range(2 * IC):
                        for c in range(DC):
                            last = t_.matmul(gate_up(e)[:, m, :], wgu[e][:, c, m * P:(m + 1) * P], xsT[:, e % 2, c, :],
                                             start=(c == 0), stop=(c == DC - 1))
                    last.then_inc(s["gu_made"], 1)
                    if e:
                        down(e - 1)
                down(E - 1)


def kernel(**inputs):
    import numpy as np
    import concourse.bacc as bacc
    from concourse.bass_utils import run_bass_kernel_spmd

    x = {k: np.ascontiguousarray(v) for k, v in inputs.items()}

    def column(v):
        return v.reshape(DC, P).T

    wg, wu, wd = (x["L0_ffn_" + n] for n in ("w_gate", "w_up", "w_down"))
    gu = np.concatenate([wg, wu], axis=1).transpose(0, 2, 1)
    dn = wd.transpose(0, 2, 1)
    arrays = {
        "x": x["x"].reshape(B * S, D), "ctx": x["ctx_1024"],
        "wq": x["L0_xattn_Wq"], "wkT": x["L0_xattn_Wk"].T, "wv": x["L0_xattn_Wv"],
        "awq": x["L0_attn_Wq"], "awk": x["L0_attn_Wk"], "awv": x["L0_attn_Wv"], "awo": x["L0_attn_Wo"],
        "vec": np.stack([column(x[n]) for n in ("L0_xattn_bq", "L0_xattn_bk", "L0_attn_ln_w", "L0_attn_ln_b")], axis=1),
        "rowv": np.concatenate([x[n] for n in ("L0_xattn_bv", "L0_attn_bo", "L0_attn_gq", "L0_attn_gk")]),
        "gwT": x["L0_ffn_gate_w"].T.reshape(DC, P, E).transpose(1, 0, 2),
        "wgu": gu.reshape(E, DC, P, 2 * I).transpose(0, 2, 1, 3),
        "wdn": dn.reshape(E, IC, P, D).transpose(0, 2, 1, 3),
    }
    arrays = {k: np.ascontiguousarray(v) for k, v in arrays.items()}
    nc = bacc.Bacc("TRN2", target_bir_lowering=False, num_devices=1)
    A = {k: nc.dram_tensor(k, v.shape, mybir.dt.from_np(v.dtype), kind="ExternalInput").ap() for k, v in arrays.items()}
    A["out"] = nc.dram_tensor("out", (B * S, D), mybir.dt.float32, kind="ExternalOutput").ap()
    program(nc, A)
    r = run_bass_kernel_spmd(nc, [arrays], core_ids=[0])
    return r.results[0]["out"].reshape(B, S, D)
```

```python
from contextlib import ExitStack

import concourse.bass as bass
from concourse import mybir

B, S, D = 8, 64, 512
KEYS = 1601
P = 128
DC = D // P
PAIRS = B // 2
FULL = KEYS // P
TAIL = KEYS - FULL * P
KT = FULL + 1
GT = 2
GROUPS = -(-KT // GT)
CHUNKS = [(0, 4), (4, 8), (8, FULL), (FULL, KT)]
NCH = len(CHUNKS)
HEADS, HD = 16, 32
HPC = P // HD
THRESH, SHARP = 0.29514, 15.0
EPS = 1e-5
NORM_EPS = 1e-12
E, I = 8, 256
IC = I // P
SLOTS = P
EROWS = 512
MAXR = -(-EROWS // SLOTS)
OWN = 2
NVEC = 4
ROWV = 2 * D + 2 * HD

STEPS = ("sum", "on", "y", "stats", "norm", "a2", "v", "q", "graw", "k", "kT", "turn", "align0", "align1", "gT", "col", "o",
         "hnorm", "h", "route", "rank")
BY_SCORES = {0: ("sum",), 1: ("on",), 2: ("y",), 3: ("stats",), 4: ("norm",), 5: ("a2",), 6: ("v", "q", "graw", "k"), 7: ("kT",),
             8: ("turn",), 9: ("align0",), 10: ("align1",), 11: ("gT",), 12: ("col",)}
BY_MAX = ("o",)
BY_SUMS = {1: ("hnorm", "h"), 2: ("route",), 3: ("rank",)}
LAST_SCORES = {0: ("sum",), 1: ("on",), 2: ("y",), 3: ("stats",), 4: ("norm",), 5: ("a2",), 6: ("v",), 8: ("q", "graw")}
LAST_MAX = ("k",)
LAST_SUMS = {0: ("kT",), 2: ("turn",)}
_B, _L = PAIRS - 2, PAIRS - 1
ENDING = ((_L, "sum"), (_B, "align0"), (_B, "align1"), (_L, "on"), (_B, "gT"), (_B, "col"), (_L, "y"), (_L, "stats"),
          (_L, "norm"), (_B, "o"), (_L, "a2"), (_B, "hnorm"), (_L, "v"), (_L, "q"), (_L, "graw"), (_L, "k"), (_B, "h"),
          (_L, "kT"), (_L, "turn"), (_L, "align0"), (_L, "align1"), (_L, "gT"), (_L, "col"), (_B, "route"), (_L, "o"),
          (_B, "rank"), (_L, "hnorm"), (_L, "h"), (_L, "route"), (_L, "rank"))
FILL = {(_L, "k"): 3, (_L, "turn"): 7, (_L, "align1"): 4, (_L, "gT"): 4, (_L, "col"): 2, (_L, "o"): 14, (_L, "h"): 4,
        (_L, "route"): 3, (_L, "rank"): 4}
TOKEN_FILL = 25
MAX_AT = {5: 0, 9: 1, 13: 2}
MOVES = KT + NCH // 2
AFTER = dict(zip(STEPS, STEPS[1:] + ("end",)))
LINKS = {"sum": 1, "stats": 2, "q": 1, "k": 1, "o": 2, "route": 5, "rank": 2}
LINK_AT = {}
ATT_LINKS = 0
for _step in STEPS:
    LINK_AT[_step] = ATT_LINKS
    ATT_LINKS += LINKS.get(_step, 0)
LINK_AT["end"] = ATT_LINKS
SOFT_LINKS = NCH + 2
COUNT_LINKS = 3
ROUND_LINKS = 4 + E


def program(nc, A):
    f32, f16, i32 = mybir.dt.float32, mybir.dt.float16, mybir.dt.int32
    ALU, ACT, AX = mybir.AluOpType, mybir.ActivationFunctionType, mybir.AxisListType
    scale = float(D) ** -0.5
    ctx = ExitStack()
    with ctx:
        def sb(name, shape, dt=f32):
            return ctx.enter_context(nc.sbuf_tensor(name + "_sb", shape, dt))

        def sem(name):
            return ctx.enter_context(nc.semaphore(name))

        CTX = sb("CTX", [P, 2 * KT * D])
        ctxb = CTX[:, :].rearrange("p (k t d) -> p k t d", k=2, t=KT)
        CT = sb("CT", [P, 2 * 2 * DC * GT * P])
        ctxT = CT[:, :].rearrange("p (a k c n) -> p a k c n", a=2, k=2, c=DC)
        iotaS = CT[:, 0:E * SLOTS]
        PR = sb("PR", [P, KEYS + KT * P])
        prow = PR[:, 0:KEYS]
        probs = PR[:, KEYS:KEYS + KT * P].rearrange("p (t q) -> p t q", t=KT)
        pick = PR[:, 0:PAIRS * E * SLOTS // 2].bitcast(f16).rearrange("p (a n) -> p a n", a=PAIRS)
        QK = sb("QK", [P, DC * B * S])
        qk = QK[:, :].rearrange("p (c n) -> p c n", c=DC)
        xsT = QK[:, 0:2 * DC * SLOTS].rearrange("p (a c n) -> p a c n", a=2, c=DC)
        hact = QK[:, 1024:1024 + 2 * IC * SLOTS].rearrange("p (a c n) -> p a c n", a=2, c=IC)
        gate_t = QK[:, 1536:1536 + IC * SLOTS].rearrange("p (c n) -> p c n", c=IC)
        WV = sb("WV", [P, DC * D])
        wv = WV[:, :].rearrange("p (c n) -> p c n", c=DC)
        AW = sb("AW", [P, 3 * DC * D])
        awq, awk, awv = (AW[:, i * DC * D:(i + 1) * DC * D].rearrange("p (c n) -> p c n", c=DC) for i in range(3))
        AO = sb("AO", [P, DC * D])
        awo = AO[:, :].rearrange("p (c n) -> p c n", c=DC)
        WQK = sb("WQK", [P, 2 * DC * D])
        wq = WQK[:, 0:DC * D].rearrange("p (c n) -> p c n", c=DC)
        wkT = WQK[:, DC * D:2 * DC * D].rearrange("p (c n) -> p c n", c=DC)
        qmask = WQK[:, 0:DC * HPC * P].rearrange("p (c j n) -> p c j n", c=DC, j=HPC)
        resbd = WQK[:, DC * D:DC * D + HEADS * P].rearrange("p (h n) -> p h n", h=HEADS)
        XW = DC * 2 * I + IC * D
        FF = sb("FF", [P, OWN * XW])
        xall = AW[:, 0:PAIRS * D].rearrange("p (a d) -> p a d", a=PAIRS)
        xn = AW[:, PAIRS * D:2 * PAIRS * D].rearrange("p (a d) -> p a d", a=PAIRS)
        xnT = AW[:, 2 * PAIRS * D:3 * PAIRS * D].rearrange("p (c n) -> p c n", c=DC)
        qpT = AO[:, :].rearrange("p (c n) -> p c n", c=DC)
        places = [(FF[:, e * XW:e * XW + DC * 2 * I], FF[:, e * XW + DC * 2 * I:(e + 1) * XW]) for e in range(OWN)]
        places += [(CTX[:, e * XW:e * XW + DC * 2 * I], CTX[:, e * XW + DC * 2 * I:(e + 1) * XW]) for e in range(4)]
        places += [(WV[:, :], CTX[:, 4 * XW:4 * XW + IC * D])]
        places += [(WQK[:, 0:DC * 2 * I], WQK[:, DC * 2 * I:XW])]
        wgu = [g.rearrange("p (c n) -> p c n", c=DC) for g, _ in places]
        wdn = [d.rearrange("p (c n) -> p c n", c=IC) for _, d in places]
        got = [(AW if e < 6 else AO)[0:SLOTS, (e % 6) * 2 * D:(e % 6 + 1) * 2 * D] for e in range(E)]

        def tile(name):
            return sb(name, [P, D])

        qcur = sb("qcur", [P, DC, P])
        xrow, x1_own, a2, sq, vs_own, qh, kh = (tile(n) for n in ("xrow", "x1", "a2", "sq", "vs", "qh", "kh"))
        on = sq
        rawT_own, normT_own = (sb(n, [P, DC, P]) for n in ("rawT", "normT"))
        gq, gqT = kh, qh[:, :].rearrange("p (c n) -> p c n", c=DC)
        x1_l, vs_l = (CT[:, E * SLOTS + i * D:E * SLOTS + (i + 1) * D] for i in range(2))
        rawT_l, normT_l = (CT[:, E * SLOTS + i * D:E * SLOTS + (i + 1) * D].rearrange("p (c n) -> p c n", c=DC) for i in range(2, 4))
        yout = [a2, kh]
        res = sb("res", [P, DC, HPC * S])
        XR_own = sb("XR", [P, 2 * D])
        XR_l = CT[:, E * SLOTS + 4 * D:E * SLOTS + 6 * D]
        wgate = sb("wgate", [P, DC, 2 * HEADS])
        gwT = sb("gwT", [P, DC, E])
        vec = sb("vec", [P, NVEC, DC])
        rowv = sb("rowv", [P, ROWV])
        bv, bo = rowv[:, 0:D], rowv[:, D:2 * D]
        ident = sb("ident", [P, P])
        before = sb("before", [P, P], f16)
        ones16 = sb("ones16", [P, P], f16)
        token = sb("token", [P, PAIRS], f16)
        desc = sb("desc", [P, E])
        ebase = sb("ebase", [P, E])
        halves = sb("halves", [P, 3])
        nhalf = sb("nhalf", [P, 2 * HEADS])
        mx = sb("mx", [P, NCH + 3])
        esum = sb("esum", [P, NCH + 2])
        call = sb("call", [P, PAIRS])
        ccur = sb("ccur", [P, 1])
        st = sb("st", [P, PAIRS, 6])
        mv = sb("mv", [P, PAIRS, 2])
        ratio = sb("ratio", [P, 1])
        rstd = sb("rstd", [P, PAIRS])
        ss = sb("ss", [P, 2 * HEADS])
        rn = sb("rn", [P, 2 * HEADS])
        graw = sb("graw", [P, 2 * HEADS])
        gates = sb("gates", [P, 2 * HEADS])
        sm = sb("sm", [P, 4])
        rt = sb("rt", [P, 2, E])
        onehot = sb("onehot", [P, E], f16)
        onesum = sb("onesum", [P, E], f16)
        slot = sb("slot", [P, PAIRS])
        cnt = sb("cnt", [P, 2 + MAXR - 1])
        limits = sb("limits", [P, MAXR - 1])
        tbias = sb("tbias", [P, 1])
        primed = sb("primed", [P, 1])
        rounds = sb("rounds", [1, 1], i32)
        tok = sb("tok", [SLOTS, 3, E])
        idxg = sb("idxg", [SLOTS, E], i32)
        idxs = sb("idxs", [SLOTS, E], i32)

        def bank(name, n=1):
            return ctx.enter_context(nc.psum_tensor(name, [P, n * 512], f32))

        TR = [bank("TR0"), bank("TR1")]
        SC = bank("SC", 3)
        ST = bank("ST")
        AB = [bank("A0"), bank("A1")]

        def is_last(p):
            return isinstance(p, int) and p == PAIRS - 1

        def places_of(p):
            if is_last(p):
                return x1_l, vs_l, rawT_l, normT_l, XR_l, TR[0], TR[1]
            return x1_own, vs_own, rawT_own, normT_own, XR_own, AB[0], AB[1]

        def gate_up(e):
            return AB[e % 2][:, 0:2 * IC * SLOTS].rearrange("p (m n) -> p m n", m=2 * IC)

        chunk_scores = [SC[:, lo * P:hi * P] for lo, hi in CHUNKS[:-1]] + [ST[:, 0:TAIL]]
        down_bank = [SC[:, 0:D], SC[:, D:2 * D]]

        scratch = nc.dram_tensor("rows", (B * S, 2 * D), f32, kind="Internal").ap()

        names = """passed x_in0 x_in1 wq_in wkT_in vec_in rowv_in wv_in aq_in ak_in av_in awo_in gwT_in
            half_made part_made const_made bias_made ln0_eps ln0_pow xn_made xnT_turned xnT_made
            qp_made qp_moved qk_made qk_moved c_made c_moved gmul gred masks_zeroed
            qcur_made ccur_made turned0 turned1 moved0 moved1 scored shift_made exp_made pv_chunk rsum_made on_made on_turned pvt_made
            x_loaded xbv_made y_made x1_made x1b_made var1 pow1
            a2_made ratio_made a2_turned rawT_made normT_made v_made v_moved q_made q_sq ssq powq qh_made
            k_made k_sq ssk powk k_moved graw_made graw_moved gates_made vp_made q_turned qmask_act qmask_dve
            k_turned kT_made al_made scaled_made res_made resbd_made col_made gq_made gq_turned gqT_made cgT_made
            o_made x2_made var3 pow3 h_made h_turned hT_made lg_made top_made en_made hot_made
            xr_made xr_free rank_made sum_hot slot_made iota_made count_made rounds_made
            pick_made tok_made idxg_made idxs_made x_turned xT_moved gu_made gate_made act_made y2_made yout_made
            pro_chain soft_chain att_chain round_chain""".split()
        s = {n: sem(n) for n in names}
        s_ctx = [[sem(f"ctx_in{k}{c}") for c in range(NCH)] for k in range(2)]
        s_w = [sem(f"expert_in{e}") for e in range(E)]
        s_got = [sem(f"rows_got{e}") for e in range(E)]
        s_stored = [sem(f"out_stored{i}") for i in range(2)]

        block = ctx.enter_context(nc.Block())

        def earlier(eng, name, n):
            if not isinstance(n, int) or n > 0:
                eng.wait_ge(s[name], n)

        def earlier_last(eng, name, n):
            if isinstance(n, int) and n > 0:
                eng.wait_ge(s[name], n)

        def settle(eng):
            eng.sem_inc(s["passed"], 1)

        def turned_bank(bank):
            return bank[:, :].rearrange("p (c n) -> p c n", c=DC)

        def move_keys(eng, copy, p, k, t):
            if t >= KT:
                return
            grp, w = t // GT, P if t < FULL else TAIL
            eng.wait_ge(s[f"turned{k}"], MOVES * p + t + 1)
            earlier(eng, "scored", GROUPS * p + (grp - 1 if grp else 0))
            copy(ctxT[:, grp % 2, k, :, (t % GT) * P:(t % GT) * P + w], turned_bank(TR[k])[:, :, 0:w]).then_inc(s[f"moved{k}"], 1)

        def move_numerators(eng, copy, p, c):
            lo, hi = CHUNKS[c]
            w = P if c < NCH - 1 else TAIL
            eng.wait_ge(s[f"turned{c % 2}"], MOVES * p + KT + c // 2 + 1)
            copy(probs[0:w, lo:hi, :], TR[c % 2][0:w, 0:(hi - lo) * P].rearrange("p (t q) -> p t q", q=P)).then_inc(s[f"moved{c % 2}"], 1)

        @block.sync
        def _(sp):
            def load_ctx(b, k, c):
                lo, hi = CHUNKS[c]
                if c < NCH - 1:
                    src = A["ctx"][bass.ds(b, 1), 0:FULL * P, :].rearrange("a (p t) d -> p (a t) d", t=FULL)[:, lo:hi, :]
                    sp.dma_start(ctxb[:, k, lo:hi, :], src).then_inc(s_ctx[k][c], 16)
                else:
                    src = A["ctx"][bass.ds(b, 1), FULL * P:KEYS, :].rearrange("a p d -> p (a d)")
                    sp.dma_start(ctxb[0:TAIL, k, FULL, :], src).then_inc(s_ctx[k][c], 16)

            def load_pair(p):
                for c in range(NCH):
                    earlier(sp, "pv_chunk", NCH * (p - 1) + c + 1)
                    for k in range(2):
                        load_ctx(2 * p + k, k, c)

            def load_weight(dst, name, signal):
                sp.dma_start(dst, A[name].rearrange("(c p) n -> p c n", p=P)).then_inc(s[signal], 16)

            def load_expert(e):
                sp.dma_start(wgu[e], A["wgu"][e]).then_inc(s_w[e], 16)
                sp.dma_start(wdn[e], A["wdn"][e]).then_inc(s_w[e], 16)

            def load_x(p):
                earlier(sp, "x1_made", p)
                sp.dma_start(xrow[:, :], A["x"][bass.ds(p * P, P), :]).then_inc(s["x_loaded"], 16)

            def store_rows(p):
                sp.wait_ge(s["xr_made"], p + 1)
                sp.dma_start(scratch[bass.ds(p * P, P), :], places_of(p)[4][:, :]).then_inc(s["xr_free"], 16)

            sp.sem_inc(s["xr_free"], 16)
            for i in range(2):
                src = A["x"][2 * i * P:(2 * i + 2) * P, :].rearrange("(a p) d -> p a d", p=P)
                sp.dma_start(xall[:, 2 * i:2 * i + 2, :], src).then_inc(s[f"x_in{i}"], 16)
            load_weight(wq, "wq", "wq_in")
            load_weight(wkT, "wkT", "wkT_in")
            load_x(0)
            load_pair(0)
            load_weight(wv, "wv", "wv_in")
            sp.wait_ge(s["qp_made"], 2 * DC)
            load_weight(awq, "awq", "aq_in")
            load_weight(awk, "awk", "ak_in")
            load_weight(awv, "awv", "av_in")
            sp.wait_ge(s["qk_made"], 2 * DC)
            sp.wait_ge(s["c_made"], 1)
            load_weight(awo, "awo", "awo_in")
            load_pair(1)
            for e in range(OWN):
                load_expert(e)
            with sp.Fori(1, PAIRS - 1) as p:
                load_x(p)
                load_pair(p + 1)
                store_rows(p - 1)
            load_x(PAIRS - 1)
            sp.wait_ge(s["pv_chunk"], NCH * PAIRS)
            for e in range(OWN, OWN + 4):
                load_expert(e)
            sp.wait_ge(s["y_made"], PAIRS)
            load_expert(OWN + 4)
            sp.wait_ge(s["col_made"], PAIRS)
            load_expert(E - 1)
            store_rows(PAIRS - 2)
            store_rows(PAIRS - 1)
            sp.wait_ge(s["xr_free"], 16 * PAIRS + 16)

        @block.gpsimd
        def _(pool):
            g = nc.gpsimd
            pool.dma_start(vec[:], A["vec"]).then_inc(s["vec_in"], 16)
            g.memset(nhalf[:], -0.5).then_inc(s["half_made"], 1)
            g.memset(ident[:], 0.0).then_inc(s["part_made"], 1)
            g.memset(before[:], 1.0).then_inc(s["part_made"], 1)
            pool.wait_ge(s["part_made"], 2)
            g.affine_select(out=ident[:], in_=ident[:], compare_op=ALU.not_equal, fill=1.0, base=0,
                            pattern=[[-1, P]], channel_multiplier=1).then_inc(s["const_made"], 1)
            g.affine_select(out=before[:], in_=before[:], compare_op=ALU.is_gt, fill=0.0, base=0,
                            pattern=[[1, P]], channel_multiplier=-1).then_inc(s["const_made"], 1)
            g.memset(ones16[:], 1.0).then_inc(s["const_made"], 1)
            g.memset(halves[:, 0:2], -0.5).then_inc(s["half_made"], 1)
            g.memset(halves[:, 2:3], 0.5).then_inc(s["half_made"], 1)
            g.memset(onesum[:], 0.0).then_inc(s["const_made"], 1)
            loose = dict(channel_multiplier=0, allow_small_or_imprecise_dtypes=True)
            g.iota(desc[:], pattern=[[-1, E]], base=E, **loose).then_inc(s["const_made"], 1)
            g.iota(ebase[:], pattern=[[EROWS, E]], base=0, **loose).then_inc(s["const_made"], 1)
            g.iota(limits[:], pattern=[[SLOTS, MAXR - 1]], base=SLOTS, **loose).then_inc(s["const_made"], 1)
            g.iota(token[:], pattern=[[P, PAIRS]], base=1, channel_multiplier=1,
                   allow_small_or_imprecise_dtypes=True).then_inc(s["const_made"], 1)
            pool.dma_start(rowv[:], A["rowv"].partition_broadcast(P)).then_inc(s["rowv_in"], 16)
            pool.dma_start(gwT[:], A["gwT"]).then_inc(s["gwT_in"], 16)
            for i in range(2):
                pool.wait_ge(s["ln0_eps"], i + 1)
                g.tensor_tensor(rstd[:, 2 * i:2 * i + 2], rstd[:, 2 * i:2 * i + 2], nhalf[:, 0:2], ALU.pow).then_inc(s["ln0_pow"], 1)

            def pair_queries(p):
                pool.wait_ge(s["qk_moved"], DC if isinstance(p, int) and p == 0 else 2 * DC)
                earlier(pool, "scored", GROUPS * p)
                g.tensor_copy(qcur[:], qk[:, :, bass.ds(p * P, P)]).then_inc(s["qcur_made"], 1)

            def pair_bias(p):
                pool.wait_ge(s["c_moved"], 1)
                earlier(pool, "shift_made", p)
                g.tensor_copy(ccur[:], call[:, bass.ds(p, 1)]).then_inc(s["ccur_made"], 1)

            def add_bv(p):
                pool.wait_ge(s["x_loaded"], 16 * p + 16)
                g.tensor_tensor(xrow[:], xrow[:], bv, ALU.add).then_inc(s["xbv_made"], 1)

            def attention(p, step):
                x1, vs, rawT, normT, XR, A0, A1 = places_of(p)
                if step == "norm":
                    pool.wait_ge(s["half_made"], 3)
                    pool.wait_ge(s["var1"], 3 * p + 3)
                    g.tensor_tensor(rstd[:, 0:3], rstd[:, 0:3], halves[:], ALU.pow).then_inc(s["pow1"], 1)
                elif step == "a2":
                    pool.wait_ge(s["a2_made"], p + 1)
                    g.tensor_tensor(x1[:, :], x1[:, :], bo, ALU.add).then_inc(s["x1b_made"], 1)
                elif step == "q":
                    pool.wait_ge(s["ssq"], p + 1)
                    g.tensor_tensor(rn[:, 0:HEADS], ss[:, 0:HEADS], nhalf[:, 0:HEADS], ALU.pow).then_inc(s["powq"], 1)
                elif step == "k":
                    pool.wait_ge(s["ssk"], p + 1)
                    g.tensor_tensor(rn[:, HEADS:], ss[:, HEADS:], nhalf[:, HEADS:], ALU.pow).then_inc(s["powk"], 1)
                elif step == "turn":
                    pool.wait_ge(s["gates_made"], p + 1)
                    pool.wait_ge(s["v_moved"], p + 1)
                    v3 = vs[:, :].rearrange("p (h d) -> p h d", h=HEADS)
                    g.tensor_tensor(v3, v3, gates[:, HEADS:].unsqueeze(2).to_broadcast([P, HEADS, HD]), ALU.mult).then_inc(s["vp_made"], 1)
                elif step == "hnorm":
                    pool.wait_ge(s["var3"], p + 1)
                    g.tensor_tensor(rstd[:, 3:4], rstd[:, 3:4], nhalf[:, 0:1], ALU.pow).then_inc(s["pow3"], 1)
                elif step == "rank" and not is_last(p):
                    pool.wait_ge(s["rank_made"], p + 1)
                    g.tensor_tensor(onesum[:], onesum[:], onehot[:], ALU.add).then_inc(s["sum_hot"], 1)

            pair_queries(0)
            pool.wait_ge(s["rowv_in"], 16)
            pool.wait_ge(s["aq_in"], 16)
            pool.wait_ge(s["ak_in"], 16)
            for n in range(2 * DC):
                w = (awq, awk)[n // DC][:, n % DC, :].rearrange("p (h d) -> p h d", h=HEADS)
                at = 2 * D + HD * (n // DC)
                gv = rowv[:, at:at + HD].unsqueeze(1).to_broadcast([P, HEADS, HD])
                if n >= 2:
                    pool.wait_ge(s["gred"], n - 1)
                g.tensor_tensor((sq, kh)[n % 2][:, :].rearrange("p (h d) -> p h d", h=HEADS), w, gv, ALU.mult).then_inc(s["gmul"], 1)
            pair_bias(0)
            pool.wait_ge(s["qk_made"], 2 * DC)
            g.memset(WQK[:], 0.0).then_inc(s["masks_zeroed"], 1)
            with pool.Fori(1, PAIRS - 1) as p:
                pair_queries(p)
                pair_bias(p)
                add_bv(p - 1)
                for step in STEPS:
                    attention(p - 1, step)
            pair_queries(PAIRS - 1)
            pair_bias(PAIRS - 1)
            add_bv(PAIRS - 2)
            for step in STEPS[:STEPS.index("turn") + 1]:
                attention(PAIRS - 2, step)
            add_bv(PAIRS - 1)
            pool.wait_ge(s["scored"], GROUPS * PAIRS)
            g.iota(iotaS.rearrange("p (e i) -> p e i", e=E), pattern=[[EROWS, E], [1, SLOTS]], base=0, **loose).then_inc(s["iota_made"], 1)
            for p, step in ENDING:
                attention(p, step)

            pool.wait_ge(s["rounds_made"], 1)
            nr = pool.value_load(rounds[0:1, 0:1], min_val=1, max_val=MAXR)
            pool.wait_ge(s["xr_free"], 16 * PAIRS + 16)
            with pool.Fori(0, nr) as r:
                pool.wait_ge(s["idxg_made"], r + 1)
                settle(pool)
                for e in range(E):
                    g.indirect_dma_start(out=got[e], out_offset=None, in_=scratch[:, :],
                                         in_offset=bass.IndirectOffsetOnAxis(ap=idxg[:, e:e + 1], axis=0)).then_inc(s_got[e], 16)
                for e in range(E):
                    if e == 0:
                        pool.wait_ge(s["idxs_made"], r + 1)
                    pool.wait_ge(s["yout_made"], E * r + e + 1)
                    settle(pool)
                    g.indirect_dma_start(out=A["out"][:, :], out_offset=bass.IndirectOffsetOnAxis(ap=idxs[:, e:e + 1], axis=0),
                                         in_=yout[e % 2][0:SLOTS, :], in_offset=None,
                                         bounds_check=B * S - 1, oob_is_err=False).then_inc(s_stored[e % 2], 16)
                for i in range(2):
                    pool.wait_ge(s_stored[i], 16 * (E // 2) * (r + 1))
                settle(pool)

        @block.scalar
        def _(act):
            a = nc.scalar

            def move_x0(t):
                act.wait_ge(s["xnT_turned"], t + 1)
                a.copy(xnT[:, :, t * P:(t + 1) * P], turned_bank(TR[t % 2])).then_inc(s["xnT_made"], 1)

            act.wait_ge(s["bias_made"], 1)
            a.activation(primed[:], tbias[:], ACT.Exp)
            for half in range(2):
                if half == 0:
                    move_x0(0)
                    move_x0(1)
                    act.wait_ge(s["vec_in"], 16)
                for m in range(DC):
                    if half == 0 and m == DC - 1:
                        move_x0(2)
                        move_x0(3)
                    act.wait_ge(s["qp_made"], DC * half + m + 1)
                    a.activation(qpT[:, m, 2 * P * half:2 * P * (half + 1)], AB[m % 2][:, 0:2 * P], ACT.Identity,
                                 bias=vec[:, 0, m:m + 1]).then_inc(s["qp_moved"], 1)

            def move_qk(first, m):
                n = slice(0, P) if first else slice(P, PAIRS * P)
                act.wait_ge(s["qk_made"], (m if first else DC + m) + 1)
                a.copy(qk[:, m, n], AB[m % 2][:, n]).then_inc(s["qk_moved"], 1)

            for m in range(DC):
                move_qk(True, m)

            def exponentials(p):
                act.wait_ge(s["shift_made"], p + 1)
                earlier(act, "pv_chunk", NCH * p)
                for c, (lo, hi) in enumerate(CHUNKS):
                    keys = slice(lo * P, min(hi * P, KEYS))
                    a.activation(prow[:, keys], chunk_scores[c], ACT.Exp, bias=mx[:, NCH + 2:NCH + 3], scale=scale,
                                 accum_out=esum[:, c:c + 1]).then_inc(s["exp_made"], 1)

            def attention(p, step):
                x1, vs, rawT, normT, XR, A0, A1 = places_of(p)
                if step == "sum":
                    act.wait_ge(s["rsum_made"], p + 1)
                    act.wait_ge(s["pv_chunk"], NCH * (p + 1))
                    a.activation(on[:], ST[:, :], ACT.Identity, scale=esum[:, NCH + 1:NCH + 2]).then_inc(s["on_made"], 1)
                elif step == "on":
                    act.wait_ge(s["on_turned"], p + 1)
                    a.copy(rawT[:, :, :], turned_bank(A1)).then_inc(s["pvt_made"], 1)
                elif step == "a2":
                    act.wait_ge(s["a2_turned"], p + 1)
                    a.copy(rawT[:, :, :], turned_bank(A1)).then_inc(s["rawT_made"], 1)
                elif step == "v":
                    act.wait_ge(s["v_made"], p + 1)
                    act.wait_ge(s["ratio_made"], p + 1)
                    a.activation(vs[:, :], A0[:, :], ACT.Identity, scale=ratio[:, 0:1]).then_inc(s["v_moved"], 1)
                elif step == "q":
                    act.wait_ge(s["q_made"], p + 1)
                    a.activation(sq[:], A1[:, :], ACT.Square).then_inc(s["q_sq"], 1)
                elif step == "k":
                    act.wait_ge(s["k_made"], p + 1)
                    a.copy(kh[:], A0[:, :]).then_inc(s["k_moved"], 1)
                    act.wait_ge(s["ssq"], p + 1)
                    a.activation(sq[:], A0[:, :], ACT.Square).then_inc(s["k_sq"], 1)
                elif step == "graw":
                    act.wait_ge(s["graw_made"], p + 1)
                    a.copy(graw[:], ST[:, 0:2 * HEADS]).then_inc(s["graw_moved"], 1)
                elif step == "kT":
                    act.wait_ge(s["k_turned"], p + 1)
                    a.copy(rawT[:, :, :], turned_bank(A0)).then_inc(s["kT_made"], 1)
                elif step == "turn":
                    act.wait_ge(s["q_turned"], p + 1)
                    for j in range(2):
                        q = slice(HD * j, HD * (j + 1))
                        a.copy(qmask[q, :, j, :], turned_bank(A1)[q, :, :]).then_inc(s["qmask_act"], 1)
                    act.wait_ge(s["gates_made"], p + 1)
                    a.copy(gq[:, :].rearrange("p (h d) -> p h d", h=HEADS),
                           gates[:, 0:HEADS].unsqueeze(2).to_broadcast([P, HEADS, HD])).then_inc(s["gq_made"], 1)
                elif step in ("align0", "align1"):
                    half = int(step[-1])
                    act.wait_ge(s["scaled_made"], 2 * p + half + 1)
                    a.activation(res[:, 2 * half:2 * half + 2, :], res[:, 2 * half:2 * half + 2, :], ACT.Tanh,
                                 scale=SHARP / 2, bias=tbias[:, 0:1]).then_inc(s["res_made"], 1)
                elif step == "gT":
                    act.wait_ge(s["gq_turned"], p + 1)
                    a.copy(gqT, turned_bank(A1)).then_inc(s["gqT_made"], 1)
                elif step == "h":
                    act.wait_ge(s["h_turned"], p + 1)
                    a.copy(normT[:, :, :], turned_bank(A1)).then_inc(s["hT_made"], 1)
                elif step == "route":
                    act.wait_ge(s["top_made"], p + 1)
                    a.activation(sm[:, 2:3], sm[:, 0:1], ACT.Exp, scale=-1.0).then_inc(s["en_made"], 1)

            for t in range(KT):
                if t == GT:
                    move_qk(False, 0)
                    move_qk(False, 1)
                move_keys(act, a.copy, 0, 0, t)
            act.wait_ge(s["c_made"], 1)
            a.copy(call[:], AB[1][:, 0:PAIRS]).then_inc(s["c_moved"], 1)
            exponentials(0)
            move_qk(False, 2)
            move_qk(False, 3)
            for c in range(0, NCH, 2):
                move_numerators(act, a.copy, 0, c)

            def pair(p, by_scores, by_max, by_sums):
                for t in range(GT):
                    move_keys(act, a.copy, p, 0, t)
                for u in range(2 * GROUPS):
                    for step in by_scores.get(u, ()):
                        attention(p - 1, step)
                    move_keys(act, a.copy, p, 0, GT + u)
                exponentials(p)
                for step in by_max:
                    attention(p - 1, step)
                move_numerators(act, a.copy, p, 0)
                for c in range(NCH):
                    for step in by_sums.get(c, ()):
                        attention(p - 1, step)
                    if c % 2 and c + 1 < NCH:
                        move_numerators(act, a.copy, p, c + 1)

            with act.Fori(1, PAIRS - 1) as p:
                pair(p, BY_SCORES, BY_MAX, BY_SUMS)
            pair(PAIRS - 1, LAST_SCORES, LAST_MAX, LAST_SUMS)
            for p, step in ENDING:
                attention(p, step)

            act.wait_ge(s["rounds_made"], 1)
            nr = act.value_load(rounds[0:1, 0:1], min_val=1, max_val=MAXR)
            with act.Fori(0, nr) as r:
                for e in range(E):
                    act.wait_ge(s["gu_made"], E * r + e + 1)
                    if e:
                        act.wait_ge(s["act_made"], E * r + e)
                    a.activation(gate_t[:], gate_up(e)[:, 0:IC, :], ACT.Tanh, scale=0.5).then_inc(s["gate_made"], 1)

        @block.vector
        def _(dve):
            v = nc.vector

            def linker(name, base):
                n = [0]

                def step(ins, settled=False):
                    n[0] += 1
                    ins.then_inc(s[name], 1)
                    dve.wait_ge(s[name], base + n[0])
                    if settled:
                        settle(dve)
                return step, n

            link, _ = linker("pro_chain", 0)
            v.memset(tbias[:], -SHARP * THRESH / 2).then_inc(s["bias_made"], 1)
            dve.wait_ge(s["half_made"], 1)
            for i in range(2):
                dve.wait_ge(s[f"x_in{i}"], 16)
                for t in range(2 * i, 2 * i + 2):
                    link(v.bn_stats(st[:, t, :], xall[:, t, :]))
                    link(v.bn_aggr(mv[:, t, :], st[:, t, :]))
                v.tensor_scalar(rstd[:, 2 * i:2 * i + 2], mv[:, 2 * i:2 * i + 2, 1], EPS, None, ALU.add).then_inc(s["ln0_eps"], 1)
                dve.wait_ge(s["ln0_pow"], i + 1)
                for t in range(2 * i, 2 * i + 2):
                    v.tensor_scalar(xn[:, t, :], xall[:, t, :], mv[:, t, 0:1], rstd[:, t:t + 1], ALU.subtract, ALU.mult).then_inc(s["xn_made"], 1)
            def maximum(p, c):
                link, _ = linker("soft_chain", SOFT_LINKS * p + c)
                dve.wait_ge(s["scored"], GROUPS * p + min(CHUNKS[c][1] // GT, GROUPS - 1) + (c == NCH - 1))
                link(v.tensor_reduce(mx[:, c:c + 1], chunk_scores[c], AX.X, ALU.max))

            def shift(p):
                maximum(p, NCH - 1)
                link, n = linker("soft_chain", SOFT_LINKS * p + NCH)
                link(v.tensor_reduce(mx[:, NCH:NCH + 1], mx[:, 0:NCH], AX.X, ALU.max))
                dve.wait_ge(s["ccur_made"], p + 1)
                link(v.tensor_tensor(mx[:, NCH + 1:NCH + 2], mx[:, NCH:NCH + 1], ccur[:], ALU.add))
                v.tensor_scalar(mx[:, NCH + 2:NCH + 3], mx[:, NCH + 1:NCH + 2], ccur[:, 0:1], -scale,
                                ALU.subtract, ALU.mult).then_inc(s["shift_made"], 1)
                assert n[0] + NCH == SOFT_LINKS

            def heads(x):
                return x[:, :].rearrange("p (h d) -> p h d", h=HEADS)

            links_made = [ATT_LINKS * (PAIRS - 2)]

            def attention(p, step):
                x1, vs, rawT, normT, XR, A0, A1 = places_of(p)

                def start(k):
                    return linker("att_chain", links_made[0] if isinstance(p, int) else ATT_LINKS * p + LINK_AT[k])

                def statistics(link, x, i):
                    link(v.bn_stats(st[:, i, :], x), settled=True)
                    link(v.bn_aggr(mv[:, i, :], st[:, i, :]))

                link, n = start(step)
                if step == "sum":
                    dve.wait_ge(s["exp_made"], NCH * (p + 1))
                    link(v.tensor_reduce(esum[:, NCH:NCH + 1], esum[:, 0:NCH], AX.X, ALU.add))
                    v.reciprocal(esum[:, NCH + 1:NCH + 2], esum[:, NCH:NCH + 1]).then_inc(s["rsum_made"], 1)
                elif step == "y":
                    dve.wait_ge(s["y_made"], p + 1)
                    dve.wait_ge(s["xbv_made"], p + 1)
                    v.tensor_tensor(x1[:, :], A0[:, :], xrow[:], ALU.add).then_inc(s["x1_made"], 1)
                elif step == "stats":
                    dve.wait_ge(s["x1_made"], p + 1)
                    statistics(link, x1[:, :], 0)
                    v.tensor_scalar(rstd[:, 0:1], mv[:, 0, 1:2], EPS, None, ALU.add).then_inc(s["var1"], 1)
                    for i in range(1, 3):
                        v.tensor_scalar(rstd[:, i:i + 1], mv[:, 0, 1:2], 1.0 + EPS, EPS * EPS, ALU.mult, ALU.add).then_inc(s["var1"], 1)
                elif step == "norm":
                    dve.wait_ge(s["pow1"], p + 1)
                    v.tensor_scalar(a2[:], x1[:, :], mv[:, 0, 0:1], rstd[:, 1:2], ALU.subtract, ALU.mult).then_inc(s["a2_made"], 1)
                    v.tensor_tensor(ratio[:], rstd[:, 0:1], rstd[:, 2:3], ALU.mult).then_inc(s["ratio_made"], 1)
                elif step == "a2":
                    dve.wait_ge(s["rawT_made"], p + 1)
                    for c in range(DC):
                        v.tensor_scalar(normT[:, c, :], rawT[:, c, :], vec[:, 2, c:c + 1], vec[:, 3, c:c + 1],
                                        ALU.mult, ALU.add).then_inc(s["normT_made"], 1)
                elif step == "q":
                    dve.wait_ge(s["q_sq"], p + 1)
                    link(v.tensor_reduce(ss[:, 0:HEADS], heads(sq), AX.X, ALU.add))
                    v.tensor_scalar(ss[:, 0:HEADS], ss[:, 0:HEADS], NORM_EPS ** 2, None, ALU.max).then_inc(s["ssq"], 1)
                elif step == "k":
                    dve.wait_ge(s["powq"], p + 1)
                    v.tensor_tensor(heads(qh), heads(A1), rn[:, 0:HEADS].unsqueeze(2).to_broadcast([P, HEADS, HD]),
                                    ALU.mult).then_inc(s["qh_made"], 1)
                    dve.wait_ge(s["k_sq"], p + 1)
                    link(v.tensor_reduce(ss[:, HEADS:], heads(sq), AX.X, ALU.add))
                    v.tensor_scalar(ss[:, HEADS:], ss[:, HEADS:], NORM_EPS ** 2, None, ALU.max).then_inc(s["ssk"], 1)
                elif step == "turn":
                    dve.wait_ge(s["masks_zeroed"], 1)
                    dve.wait_ge(s["q_turned"], p + 1)
                    for j in range(2, HPC):
                        q = slice(HD * j, HD * (j + 1))
                        v.tensor_copy(qmask[q, :, j, :], turned_bank(A1)[q, :, :]).then_inc(s["qmask_dve"], 1)
                    dve.wait_ge(s["powk"], p + 1)
                    dve.wait_ge(s["graw_moved"], p + 1)
                    v.tensor_tensor(gates[:], graw[:], rn[:], ALU.mult).then_inc(s["gates_made"], 1)
                elif step in ("align0", "align1"):
                    half = int(step[-1])
                    hs = HEADS // 2
                    dve.wait_ge(s["al_made"], 2 * p + half + 1)
                    v.tensor_tensor(res[:, 2 * half:2 * half + 2, :].rearrange("p c (j t) -> p (c j) t", t=S),
                                    (A0, A1)[half][:, :].rearrange("p (h t) -> p h t", t=S),
                                    rn[:, HEADS + hs * half:HEADS + hs * (half + 1)].unsqueeze(2).to_broadcast([P, hs, S]),
                                    ALU.mult).then_inc(s["scaled_made"], 1)
                elif step == "gT":
                    hs = HEADS // 2
                    for h in range(2):
                        dve.wait_ge(s["res_made"], 2 * p + h + 1)
                        for k in range(2):
                            q = slice(S * k, S * (k + 1))
                            v.tensor_scalar(resbd[q, hs * h:hs * (h + 1), q],
                                            res[q, 2 * h:2 * h + 2, :].rearrange("p c (j t) -> p (c j) t", t=S),
                                            1.0, 0.5, ALU.add, ALU.mult).then_inc(s["resbd_made"], 1)
                elif step == "col":
                    dve.wait_ge(s["col_made"], p + 1)
                    dve.wait_ge(s["gqT_made"], p + 1)
                    v.tensor_tensor(rawT[:, :, :], turned_bank(A0), gqT, ALU.mult).then_inc(s["cgT_made"], 1)
                elif step == "o":
                    dve.wait_ge(s["o_made"], p + 1)
                    dve.wait_ge(s["x1b_made"], p + 1)
                    if not is_last(p):
                        dve.wait_ge(s["xr_free"], 16 * p + 16)
                    v.tensor_tensor(XR[:, D:], A0[:, :], x1[:, :], ALU.add).then_inc(s["x2_made"], 1)
                    dve.wait_ge(s["x2_made"], p + 1)
                    statistics(link, XR[:, D:], 1)
                    v.tensor_scalar(rstd[:, 3:4], mv[:, 1, 1:2], EPS, None, ALU.add).then_inc(s["var3"], 1)
                elif step == "hnorm":
                    dve.wait_ge(s["pow3"], p + 1)
                    v.tensor_scalar(XR[:, 0:D], XR[:, D:], mv[:, 1, 0:1], rstd[:, 3:4], ALU.subtract, ALU.mult).then_inc(s["h_made"], 1)
                elif step == "route":
                    dve.wait_ge(s["lg_made"], p + 1)
                    v.tensor_reduce(sm[:, 0:1], A0[:, 0:E], AX.X, ALU.max).then_inc(s["top_made"], 1)
                    dve.wait_ge(s["top_made"], p + 1)
                    link(v.tensor_scalar(rt[:, 0, :], A0[:, 0:E], sm[:, 0:1], None, ALU.is_equal))
                    link(v.tensor_tensor(rt[:, 0, :], rt[:, 0, :], desc[:], ALU.mult))
                    link(v.tensor_reduce(sm[:, 1:2], rt[:, 0, :], AX.X, ALU.max))
                    v.tensor_scalar(onehot[:], rt[:, 0, :], sm[:, 1:2], None, ALU.is_equal).then_inc(s["hot_made"], 1)
                    dve.wait_ge(s["en_made"], p + 1)
                    link(v.tensor_scalar(sm[:, 2:3], sm[:, 2:3], 1.0, None, ALU.add))
                    link(v.reciprocal(sm[:, 3:4], sm[:, 2:3]))
                    dve.wait_ge(s["h_turned"], p + 1)
                    v.tensor_scalar(XR[:, 0:D], XR[:, 0:D], sm[:, 3:4], None, ALU.mult).then_inc(s["xr_made"], 1)
                elif step == "rank":
                    dve.wait_ge(s["rank_made"], p + 1)
                    link(v.tensor_tensor(rt[:, 1, :], A1[:, 0:E], ebase[:], ALU.add))
                    link(v.tensor_tensor(rt[:, 1, :], rt[:, 1, :], onehot[:], ALU.mult))
                    v.tensor_reduce(slot[:, bass.ds(p, 1)], rt[:, 1, :], AX.X, ALU.add).then_inc(s["slot_made"], 1)
                    if not is_last(p):
                        dve.wait_ge(s["sum_hot"], p + 1)
                assert LINK_AT[step] + n[0] == LINK_AT[AFTER[step]]
                if isinstance(p, int):
                    links_made[0] += n[0]

            def choose(i):
                v.tensor_scalar(pick[:, i, :], iotaS, slot[:, i:i + 1], None, ALU.is_equal).then_inc(s["pick_made"], 1)

            dve.wait_ge(s["const_made"], 8)
            dve.wait_ge(s["vec_in"], 16)
            for t in range(GT):
                move_keys(dve, v.tensor_copy, 0, 1, t)
            for u in range(2 * GROUPS):
                if u in MAX_AT:
                    maximum(0, MAX_AT[u])
                move_keys(dve, v.tensor_copy, 0, 1, GT + u)
                n = u - (2 * GROUPS - 1 - 2 * DC)
                if 0 <= n < 2 * DC:
                    dve.wait_ge(s["gmul"], n + 1)
                    at = HEADS * (n // DC)
                    v.tensor_reduce(wgate[:, n % DC, at:at + HEADS], (sq, kh)[n % 2][:, :].rearrange("p (h d) -> p h d", h=HEADS),
                                    AX.X, ALU.add).then_inc(s["gred"], 1)
            shift(0)
            for c in range(1, NCH, 2):
                move_numerators(dve, v.tensor_copy, 0, c)

            def pair(p, by_scores, by_max, by_sums):
                for t in range(GT):
                    move_keys(dve, v.tensor_copy, p, 1, t)
                for u in range(2 * GROUPS):
                    for step in by_scores.get(u, ()):
                        attention(p - 1, step)
                    if u in MAX_AT:
                        maximum(p, MAX_AT[u])
                    move_keys(dve, v.tensor_copy, p, 1, GT + u)
                shift(p)
                for step in by_max:
                    attention(p - 1, step)
                for c in range(NCH):
                    if c % 2 == 0:
                        move_numerators(dve, v.tensor_copy, p, c + 1)
                    for step in by_sums.get(c, ()):
                        attention(p - 1, step)

            with dve.Fori(1, PAIRS - 1) as p:
                pair(p, BY_SCORES, BY_MAX, BY_SUMS)
            pair(PAIRS - 1, LAST_SCORES, LAST_MAX, LAST_SUMS)
            for p, step in ENDING:
                attention(p, step)
                if (p, step) == (PAIRS - 1, "a2"):
                    dve.wait_ge(s["pv_chunk"], NCH * PAIRS)
                    dve.wait_ge(s["slot_made"], PAIRS - 2)
                    dve.wait_ge(s["iota_made"], 1)
                    for i in range(PAIRS - 2):
                        choose(i)
                elif (p, step) == (PAIRS - 1, "hnorm"):
                    dve.wait_ge(s["slot_made"], PAIRS - 1)
                    choose(PAIRS - 2)
            dve.wait_ge(s["slot_made"], PAIRS)
            choose(PAIRS - 1)

            link, n = linker("round_chain", 0)
            dve.wait_ge(s["count_made"], 1)
            link(v.tensor_reduce(cnt[:, 0:1], AB[1][:, 0:E], AX.X, ALU.max))
            link(v.tensor_scalar(cnt[:, 2:2 + MAXR - 1], limits[:], cnt[:, 0:1], None, ALU.is_lt))
            link(v.tensor_reduce(cnt[:, 1:2], cnt[:, 2:2 + MAXR - 1], AX.X, ALU.add))
            v.tensor_scalar(rounds[0:1, 0:1], cnt[0:1, 1:2], 1.0, None, ALU.add).then_inc(s["rounds_made"], 1)
            assert n[0] == COUNT_LINKS
            dve.wait_ge(s["rounds_made"], 1)
            nr = dve.value_load(rounds[0:1, 0:1], min_val=1, max_val=MAXR)
            with dve.Fori(0, nr) as r:
                link, n = linker("round_chain", COUNT_LINKS + ROUND_LINKS * r)
                dve.wait_ge(s["tok_made"], r + 1)
                link(v.tensor_reduce(tok[:, 2, :], ST[0:SLOTS, 0:PAIRS * E].rearrange("p (i e) -> p e i", i=PAIRS), AX.X, ALU.add))
                v.tensor_scalar(idxg[:], tok[:, 2, :], -1.0, 0.0, ALU.add, ALU.max).then_inc(s["idxg_made"], 1)
                link(v.tensor_scalar(tok[:, 0, :], tok[:, 2, :], 0.0, 2.0 * B * S, ALU.is_equal, ALU.mult))
                link(v.tensor_scalar(tok[:, 1, :], tok[:, 2, :], -1.0, None, ALU.add))
                v.tensor_tensor(idxs[:], tok[:, 0, :], tok[:, 1, :], ALU.add).then_inc(s["idxs_made"], 1)
                dve.wait_ge(s["pick_made"], PAIRS * r + PAIRS)
                link(v.tensor_scalar(slot[:], slot[:], float(-SLOTS), None, ALU.add))

                def move_x(e):
                    dve.wait_ge(s["x_turned"], E * r + e + 1)
                    if e >= 2:
                        dve.wait_ge(s["gu_made"], E * r + e - 1)
                    v.tensor_copy(xsT[:, e % 2, :, :], TR[e % 2][:, 0:DC * SLOTS].rearrange("p (c n) -> p c n", c=DC)).then_inc(s["xT_moved"], 1)

                def finish(e):
                    dve.wait_ge(s["y2_made"], E * r + e + 1)
                    if e >= 2:
                        dve.wait_ge(s_stored[e % 2], 16 * ((E // 2) * r + e // 2))
                    v.tensor_tensor(yout[e % 2][0:SLOTS, :], down_bank[e % 2][0:SLOTS, :], got[e][:, D:], ALU.add).then_inc(s["yout_made"], 1)

                move_x(0)
                for e in range(E):
                    if e + 1 < E:
                        move_x(e + 1)
                    dve.wait_ge(s["gate_made"], E * r + e + 1)
                    link(v.scalar_tensor_tensor(out=gate_t[:], in0=gate_t[:], scalar=1.0, in1=gate_up(e)[:, 0:IC, :], op0=ALU.add, op1=ALU.mult))
                    v.scalar_tensor_tensor(out=hact[:, e % 2, :, :], in0=gate_t[:], scalar=0.5, in1=gate_up(e)[:, IC:, :],
                                           op0=ALU.mult, op1=ALU.mult).then_inc(s["act_made"], 1)
                    if e:
                        finish(e - 1)
                    if e < PAIRS:
                        choose(e)
                finish(E - 1)
                for i in range(2):
                    dve.wait_ge(s_stored[i], 16 * (E // 2) * (r + 1))
                assert n[0] == ROUND_LINKS

        @block.tensor
        def _(pe):
            t_ = nc.tensor
            pe.wait_ge(s["const_made"], 8)

            def turn_rows(bank, rows, n, w=P):
                for c in range(DC):
                    last = t_.transpose(bank[:, c * w:c * w + n], rows[:, c * P:(c + 1) * P], ident[0:n, 0:n])
                return last

            def project(bank, left, right):
                for c in range(DC):
                    last = t_.matmul(bank[:, :], left[:, c, :], right[:, c, :], start=(c == 0), stop=(c == DC - 1))
                return last

            def turn_x0(t):
                pe.wait_ge(s["xn_made"], t + 1)
                earlier(pe, "xnT_made", t - 1)
                turn_rows(TR[t % 2], xn[:, t, :], P).then_inc(s["xnT_turned"], 1)
            for half in range(2):
                if half == 0:
                    turn_x0(0)
                    turn_x0(1)
                pe.wait_ge(s["wq_in"], 16)
                pe.wait_ge(s["xnT_made"], 2 * half + 2)
                for m in range(DC):
                    if half == 0 and m == DC - 1:
                        turn_x0(2)
                        turn_x0(3)
                    earlier(pe, "qp_moved", DC * half + m - 1)
                    for c in range(DC):
                        last = t_.matmul(AB[m % 2][:, 0:2 * P], wq[:, c, m * P:(m + 1) * P], xnT[:, c, 2 * P * half:2 * P * (half + 1)],
                                         start=(c == 0), stop=(c == DC - 1))
                    last.then_inc(s["qp_made"], 1)
            def turn_keys(p, t):
                if t >= KT:
                    return
                w = P if t < FULL else TAIL
                for k in range(2):
                    for c, (lo, _) in enumerate(CHUNKS):
                        if t == lo:
                            pe.wait_ge(s_ctx[k][c], 16 * p + 16)
                    earlier(pe, f"moved{k}", MOVES * p + t)
                    turn_rows(TR[k], ctxb[0:w, k, t, :], w, P).then_inc(s[f"turned{k}"], 1)

            def bring(first, m):
                n = slice(0, P) if first else slice(P, PAIRS * P)
                k = m if first else DC + m
                earlier(pe, "qk_moved", k - 1)
                for c in range(DC):
                    last = t_.matmul(AB[m % 2][:, n], wkT[:, c, m * P:(m + 1) * P], qpT[:, c, n], start=(c == 0), stop=(c == DC - 1))
                last.then_inc(s["qk_made"], 1)

            turn_keys(0, 0)
            pe.wait_ge(s["wkT_in"], 16)
            pe.wait_ge(s["qp_moved"], 2 * DC)
            for m in range(DC):
                bring(True, m)

            def score(p, grp, half):
                lo, n = grp * GT, GT * P if grp < GROUPS - 1 else TAIL
                if half == 0:
                    for k in range(2):
                        pe.wait_ge(s[f"moved{k}"], MOVES * p + min(lo + GT, KT))
                    if grp == 0:
                        pe.wait_ge(s["qcur_made"], p + 1)
                        earlier(pe, "exp_made", NCH * p)
                    if grp == GROUPS - 1:
                        earlier(pe, "graw_moved", p)
                out = SC[:, lo * P:lo * P + n] if grp < GROUPS - 1 else ST[:, 0:n]
                for c in range(2 * half, 2 * half + 2):
                    for k in range(2):
                        q = slice(k * S, (k + 1) * S)
                        last = t_.matmul(out[q, :], qcur[:, c, q], ctxT[:, grp % 2, k, c, 0:n], start=(c == 0), stop=(c == DC - 1))
                if half == 1:
                    last.then_inc(s["scored"], 1)

            def turn_numerators(p, c):
                lo, hi = CHUNKS[c]
                pe.wait_ge(s["exp_made"], NCH * p + c + 1)
                pe.wait_ge(s[f"moved{c % 2}"], MOVES * p + KT + c // 2)
                for t in range(lo, hi):
                    w = P if t < FULL else TAIL
                    last = t_.transpose(TR[c % 2][0:w, (t - lo) * P:(t - lo + 1) * P], prow[:, t * P:t * P + w], ident[:, :])
                last.then_inc(s[f"turned{c % 2}"], 1)

            def weigh(p, c):
                lo, hi = CHUNKS[c]
                pe.wait_ge(s[f"moved{c % 2}"], MOVES * p + KT + c // 2 + 1)
                if c == 0:
                    pe.wait_ge(s["exp_made"], NCH * (p + 1))
                for t in range(lo, hi):
                    w = P if t < FULL else TAIL
                    for k in range(2):
                        q = slice(k * S, (k + 1) * S)
                        last = t_.matmul(ST[q, :], probs[0:w, t, q], ctxb[0:w, k, t, :], start=(t == 0), stop=(t == KT - 1))
                last.then_inc(s["pv_chunk"], 1)

            def attention(p, step):
                x1, vs, rawT, normT, XR, A0, A1 = places_of(p)
                if step == "on":
                    pe.wait_ge(s["on_made"], p + 1)
                    turn_rows(A1, on, P).then_inc(s["on_turned"], 1)
                elif step == "y":
                    pe.wait_ge(s["pvt_made"], p + 1)
                    pe.wait_ge(s["wv_in"], 16)
                    project(A0, rawT, wv).then_inc(s["y_made"], 1)
                elif step == "a2":
                    pe.wait_ge(s["a2_made"], p + 1)
                    turn_rows(A1, a2, P).then_inc(s["a2_turned"], 1)
                elif step == "v":
                    pe.wait_ge(s["rawT_made"], p + 1)
                    pe.wait_ge(s["av_in"], 16)
                    project(A0, rawT, awv).then_inc(s["v_made"], 1)
                elif step == "q":
                    pe.wait_ge(s["normT_made"], DC * p + DC)
                    project(A1, normT, awq).then_inc(s["q_made"], 1)
                elif step == "k":
                    pe.wait_ge(s["v_moved"], p + 1)
                    project(A0, normT, awk).then_inc(s["k_made"], 1)
                elif step == "graw":
                    pe.wait_ge(s["gred"], 2 * DC)
                    for c in range(DC):
                        last = t_.matmul(ST[:, 0:2 * HEADS], normT[:, c, :], wgate[:, c, :], start=(c == 0), stop=(c == DC - 1))
                    last.then_inc(s["graw_made"], 1)
                elif step == "kT":
                    pe.wait_ge(s["k_moved"], p + 1)
                    pe.wait_ge(s["k_sq"], p + 1)
                    turn_rows(A0, kh, P).then_inc(s["k_turned"], 1)
                elif step == "turn":
                    pe.wait_ge(s["qh_made"], p + 1)
                    turn_rows(A1, qh, P).then_inc(s["q_turned"], 1)
                elif step in ("align0", "align1"):
                    half = int(step[-1])
                    if half == 0:
                        pe.wait_ge(s["qmask_act"], 2 * p + 2)
                        pe.wait_ge(s["qmask_dve"], 2 * p + 2)
                        pe.wait_ge(s["kT_made"], p + 1)
                    for c in range(2 * half, 2 * half + 2):
                        for k in range(2):
                            q = slice(S * k, S * (k + 1))
                            at = (c % 2) * HPC * S
                            last = t_.matmul((A0, A1)[half][q, at:at + HPC * S], rawT[:, c, q], qmask[:, c, :, q], start=True, stop=True)
                    last.then_inc(s["al_made"], 1)
                elif step == "gT":
                    pe.wait_ge(s["gq_made"], p + 1)
                    pe.wait_ge(s["scaled_made"], 2 * p + 2)
                    turn_rows(A1, gq, P).then_inc(s["gq_turned"], 1)
                elif step == "col":
                    pe.wait_ge(s["resbd_made"], 4 * p + 4)
                    pe.wait_ge(s["vp_made"], p + 1)
                    for h in range(HEADS):
                        c, j = h // HPC, h % HPC
                        last = t_.matmul(A0[HD * j:HD * (j + 1), c * P:(c + 1) * P], vs[:, HD * h:HD * (h + 1)], resbd[:, h, :],
                                         start=True, stop=True)
                    last.then_inc(s["col_made"], 1)
                elif step == "o":
                    pe.wait_ge(s["cgT_made"], p + 1)
                    pe.wait_ge(s["awo_in"], 16)
                    project(A0, rawT, awo).then_inc(s["o_made"], 1)
                elif step == "h":
                    pe.wait_ge(s["h_made"], p + 1)
                    turn_rows(A1, XR, P).then_inc(s["h_turned"], 1)
                elif step == "route":
                    pe.wait_ge(s["hT_made"], p + 1)
                    pe.wait_ge(s["gwT_in"], 16)
                    for c in range(DC):
                        last = t_.matmul(A0[:, 0:E], normT[:, c, :], gwT[:, c, :], start=(c == 0), stop=(c == DC - 1))
                    last.then_inc(s["lg_made"], 1)
                elif step == "rank":
                    pe.wait_ge(s["hot_made"], p + 1)
                    earlier_last(pe, "sum_hot", p)
                    t_.matmul(A1[:, 0:E], before[:], onehot[:], start=True, stop=False)
                    t_.matmul(A1[:, 0:E], ones16[:], onesum[:], start=False, stop=True).then_inc(s["rank_made"], 1)
                    if is_last(p):
                        t_.matmul(AB[1][:, 0:E], ones16[:], onesum[:], start=True, stop=False)
                        t_.matmul(AB[1][:, 0:E], ones16[:], onehot[:], start=False, stop=True).then_inc(s["count_made"], 1)

            def scores(p, by_scores):
                first = isinstance(p, int) and p == 0
                if not first:
                    turn_keys(p, 0)
                turn_keys(p, 1)
                if first:
                    bring(False, 0)
                    bring(False, 1)
                for u in range(2 * GROUPS):
                    for step in by_scores.get(u, ()):
                        attention(p - 1, step)
                    turn_keys(p, GT + u)
                    score(p, u // 2, u % 2)

            def sums(p, by_max, by_sums):
                for step in by_max:
                    attention(p - 1, step)
                turn_numerators(p, 0)
                for c in range(NCH):
                    if c + 1 < NCH:
                        turn_numerators(p, c + 1)
                    for step in by_sums.get(c, ()):
                        attention(p - 1, step)
                    weigh(p, c)

            scores(0, {})
            pe.wait_ge(s["qk_moved"], DC + 2)
            pe.wait_ge(s["vec_in"], 16)
            for p in range(PAIRS):
                for c in range(DC):
                    last = t_.matmul(AB[1][:, p:p + 1], qpT[:, c, p * P:(p + 1) * P], vec[:, 1, c:c + 1], start=(c == 0), stop=(c == DC - 1))
            last.then_inc(s["c_made"], 1)
            bring(False, 2)
            pe.wait_ge(s["c_moved"], 1)
            bring(False, 3)
            sums(0, (), {})
            with pe.Fori(1, PAIRS - 1) as p:
                scores(p, BY_SCORES)
                sums(p, BY_MAX, BY_SUMS)
            scores(PAIRS - 1, LAST_SCORES)
            sums(PAIRS - 1, LAST_MAX, LAST_SUMS)

            def find_tokens(r, i):
                pe.wait_ge(s["pick_made"], PAIRS * r + i + 1)
                for e in range(E):
                    last = t_.matmul(ST[0:SLOTS, i * E + e:i * E + e + 1], pick[:, i, e * SLOTS:(e + 1) * SLOTS], token[:, i:i + 1],
                                     start=True, stop=True)
                if i == PAIRS - 1:
                    last.then_inc(s["tok_made"], 1)

            def keep_clock(n):
                for _ in range(n):
                    t_.matmul(SC[:, 2 * D:2 * D + P], ident[:], ident[:], start=True, stop=True)

            pe.wait_ge(s["exp_made"], NCH * PAIRS)
            for p, step in ENDING:
                attention(p, step)
                keep_clock(FILL.get((p, step), 0))
                if (p, step) == (PAIRS - 1, "route"):
                    for i in range(PAIRS - 1):
                        find_tokens(0, i)
            find_tokens(0, PAIRS - 1)
            keep_clock(TOKEN_FILL)
            pe.wait_ge(s["rounds_made"], 1)
            nr = pe.value_load(rounds[0:1, 0:1], min_val=1, max_val=MAXR)
            with pe.Fori(0, nr) as r:
                def turn_x(e):
                    pe.wait_ge(s_got[e], 16 * r + 16)
                    if e >= 2:
                        pe.wait_ge(s["xT_moved"], E * r + e - 1)
                    turn_rows(TR[e % 2], got[e], SLOTS, SLOTS).then_inc(s["x_turned"], 1)

                def down(e):
                    pe.wait_ge(s["act_made"], E * r + e + 1)
                    if e >= 2:
                        pe.wait_ge(s["yout_made"], E * r + e - 1)
                    for c in range(IC):
                        last = t_.matmul(down_bank[e % 2][0:SLOTS, :], hact[:, e % 2, c, :], wdn[e][:, c, :],
                                         start=(c == 0), stop=(c == IC - 1))
                    last.then_inc(s["y2_made"], 1)

                turn_x(0)
                for e in range(E):
                    if e >= E - PAIRS:
                        if e == E - PAIRS:
                            pe.wait_ge(s["idxs_made"], r + 1)
                        find_tokens(r + 1, e - (E - PAIRS))
                    pe.wait_ge(s_w[e], 32)
                    pe.wait_ge(s["xT_moved"], E * r + e + 1)
                    if e >= 2:
                        pe.wait_ge(s["act_made"], E * r + e - 1)
                    for m in range(2 * IC):
                        if m == IC and e + 1 < E:
                            turn_x(e + 1)
                        for c in range(DC):
                            last = t_.matmul(gate_up(e)[:, m, :], wgu[e][:, c, m * P:(m + 1) * P], xsT[:, e % 2, c, :],
                                             start=(c == 0), stop=(c == DC - 1))
                    last.then_inc(s["gu_made"], 1)
                    if e:
                        down(e - 1)
                down(E - 1)


def kernel(**inputs):
    import numpy as np
    import concourse.bacc as bacc
    from concourse.bass_utils import run_bass_kernel_spmd

    x = {k: np.ascontiguousarray(v) for k, v in inputs.items()}

    def column(v):
        return v.reshape(DC, P).T

    wg, wu, wd = (x["L0_ffn_" + n] for n in ("w_gate", "w_up", "w_down"))
    gu = np.concatenate([wg, wu], axis=1).transpose(0, 2, 1)
    dn = wd.transpose(0, 2, 1)
    arrays = {
        "x": x["x"].reshape(B * S, D), "ctx": x["ctx_1024"],
        "wq": x["L0_xattn_Wq"], "wkT": x["L0_xattn_Wk"].T, "wv": x["L0_xattn_Wv"],
        "awq": x["L0_attn_Wq"], "awk": x["L0_attn_Wk"], "awv": x["L0_attn_Wv"], "awo": x["L0_attn_Wo"],
        "vec": np.stack([column(x[n]) for n in ("L0_xattn_bq", "L0_xattn_bk", "L0_attn_ln_w", "L0_attn_ln_b")], axis=1),
        "rowv": np.concatenate([x[n] for n in ("L0_xattn_bv", "L0_attn_bo", "L0_attn_gq", "L0_attn_gk")]),
        "gwT": x["L0_ffn_gate_w"].T.reshape(DC, P, E).transpose(1, 0, 2),
        "wgu": gu.reshape(E, DC, P, 2 * I).transpose(0, 2, 1, 3),
        "wdn": dn.reshape(E, IC, P, D).transpose(0, 2, 1, 3),
    }
    arrays = {k: np.ascontiguousarray(v) for k, v in arrays.items()}
    nc = bacc.Bacc("TRN2", target_bir_lowering=False, num_devices=1)
    A = {k: nc.dram_tensor(k, v.shape, mybir.dt.from_np(v.dtype), kind="ExternalInput").ap() for k, v in arrays.items()}
    A["out"] = nc.dram_tensor("out", (B * S, D), mybir.dt.float32, kind="ExternalOutput").ap()
    program(nc, A)
    r = run_bass_kernel_spmd(nc, [arrays], core_ids=[0])
    return r.results[0]["out"].reshape(B, S, D)
```
